# Optimizing a Trainium2 kernel written in Bass

```python
import numpy as np
import jax
import jax.numpy as jnp

def _softmax(x, axis=-1):
    return jax.nn.softmax(x, axis=axis)

def _gelu(x):
    return jax.nn.gelu(x, approximate=True)

def _silu(x):
    return jax.nn.silu(x)

def _sigmoid(x):
    return jax.nn.sigmoid(x)

def _layernorm(x, axis=-1, eps=1e-05):
    m = jnp.mean(x, axis=axis, keepdims=True)
    v = jnp.var(x, axis=axis, keepdims=True)
    return (x - m) / jnp.sqrt(v + eps)

def _scatter_add(tgt, idx, src, axis=0):
    return tgt.at[idx].add(src)

def _segment_sum(src, seg, n):
    return jax.ops.segment_sum(src, seg, n)
kernel_name = 'mk_seq_postln_d1_jaxref_r4_fd8ac3'

def setup_inputs(seed: int=0):
    np.random.seed(seed)
    _w = jnp.asarray

    def _L0_attn_setup():
        import jax, jax.numpy as jnp
        import numpy as np
        B, T, D = (1, 512, 512)
        H, DK, DV, M = (16, 64, 128, 64)
        KEY_DIM, VALUE_DIM = (H * DK, H * DV)
        EPS = 1e-05
        CLAMP_MIN, CLAMP_MAX = (-32.0, 32.0)
        XAVIER_GAIN = 2.0 ** (-2.5)

        def _chunk_abc(q, k, v, s):
            scale = q.shape[-1] ** (-0.5)
            z = jax.lax.cumlogsumexp(s, axis=2)
            g = jnp.exp(jnp.concatenate([z[:, :, :1], z[:, :, :-1]], axis=2) - z)
            p = jnp.exp(s - z)
            tfirst = lambda x: jnp.moveaxis(x, 2, 0)
            qT, kT, vT, pT, gT = map(tfirst, (q * scale, k, v, p, g))
            b, h = (q.shape[0], q.shape[1])
            hk0 = jnp.zeros((b, h, q.shape[-1], s.shape[-1]), q.dtype)

            def step_k(hk, x):
                q_t, k_t, p_t, g_t = x
                hk = hk * g_t[:, :, None, :] + k_t[..., None] * p_t[:, :, None, :]
                return (hk, jnp.einsum('bhk,bhkm->bhm', q_t, hk))
            _, okT = jax.lax.scan(step_k, hk0, (qT, kT, pT, gT))
            pvT = jax.nn.softmax(okT, axis=-1)
            hv0 = jnp.zeros((b, h, s.shape[-1], v.shape[-1]), q.dtype)

            def step_v(hv, x):
                pv_t, v_t, p_t, g_t = x
                hv = hv * g_t[..., None] + p_t[..., None] * v_t[:, :, None, :]
                return (hv, jnp.einsum('bhm,bhmv->bhv', pv_t, hv))
            _, ovT = jax.lax.scan(step_v, hv0, (pvT, vT, pT, gT))
            return jnp.moveaxis(ovT, 0, 2)
        key = jax.random.key(seed)
        ks = jax.random.split(key, 8)

        def w(k, fan_in, fan_out):
            std = XAVIER_GAIN * np.sqrt(2.0 / (fan_in + fan_out))
            return jax.random.normal(k, (fan_in, fan_out), jnp.float32) * std
        return {'hidden_states': jax.random.normal(ks[0], (B, T, D), jnp.float32), 'Wq': w(ks[1], D, KEY_DIM), 'Wk': w(ks[2], D, KEY_DIM), 'Wv': w(ks[3], D, VALUE_DIM), 'Wg': w(ks[4], D, VALUE_DIM), 'Ws': w(ks[5], D, H * M), 'Wo': w(ks[6], VALUE_DIM, D), 'g_norm_weight': jnp.ones((DV,), jnp.float32)}
    _L0_attn_in = _L0_attn_setup()

    def _L0_ffn_setup():
        import jax, jax.numpy as jnp
        import numpy as np
        B, S, D, H = (4, 512, 512, 2048)

        def fwht(x):
            orig_shape = x.shape
            n = orig_shape[-1]
            x = x.reshape(-1, n)
            h = 1
            while h < n:
                xb = x.reshape(-1, n // (2 * h), 2, h)
                a = xb[:, :, 0, :]
                b = xb[:, :, 1, :]
                x = jnp.stack([a + b, a - b], axis=2).reshape(-1, n)
                h *= 2
            scale = jnp.asarray(1.0 / np.sqrt(n), dtype=x.dtype)
            return (x * scale).reshape(orig_shape)
        key = jax.random.key(seed)
        kx, k1, k2, k3 = jax.random.split(key, 4)
        x = jax.random.normal(kx, (B, S, D), dtype=jnp.float32)
        W1 = jax.random.normal(k1, (H, D), dtype=jnp.float32) * (1.0 / np.sqrt(D))
        W2 = jax.random.normal(k2, (D, H), dtype=jnp.float32) * (1.0 / np.sqrt(H))
        W3 = jax.random.normal(k3, (H, D), dtype=jnp.float32) * (1.0 / np.sqrt(D))
        return {'x': x, 'W1': W1, 'W2': W2, 'W3': W3}
    _L0_ffn_in = _L0_ffn_setup()
    _d = {'L0_attn_hidden_states': _L0_attn_in['hidden_states'], 'L0_attn_Wq': _L0_attn_in['Wq'], 'L0_attn_Wk': _L0_attn_in['Wk'], 'L0_attn_Wv': _L0_attn_in['Wv'], 'L0_attn_Wg': _L0_attn_in['Wg'], 'L0_attn_Ws': _L0_attn_in['Ws'], 'L0_attn_Wo': _L0_attn_in['Wo'], 'L0_attn_g_norm_weight': _L0_attn_in['g_norm_weight'], 'L0_ffn_W1': _L0_ffn_in['W1'], 'L0_ffn_W2': _L0_ffn_in['W2'], 'L0_ffn_W3': _L0_ffn_in['W3']}
    _x0 = _d['L0_attn_hidden_states']
    _d['L0_attn_hidden_states'] = jax.random.normal(jax.random.fold_in(jax.random.key(seed), 1), (2, 2048, 512), dtype=_x0.dtype)
    del _x0
    return _d

def reference(L0_attn_hidden_states, L0_attn_Wq, L0_attn_Wk, L0_attn_Wv, L0_attn_Wg, L0_attn_Ws, L0_attn_Wo, L0_attn_g_norm_weight, L0_ffn_W1, L0_ffn_W2, L0_ffn_W3):

    def _L0_attn_ref(hidden_states, Wq, Wk, Wv, Wg, Ws, Wo, g_norm_weight):
        import jax, jax.numpy as jnp
        import numpy as np
        B, T, D = (1, 512, 512)
        H, DK, DV, M = (16, 64, 128, 64)
        KEY_DIM, VALUE_DIM = (H * DK, H * DV)
        EPS = 1e-05
        CLAMP_MIN, CLAMP_MAX = (-32.0, 32.0)
        XAVIER_GAIN = 2.0 ** (-2.5)

        def _chunk_abc(q, k, v, s):
            scale = q.shape[-1] ** (-0.5)
            z = jax.lax.cumlogsumexp(s, axis=2)
            g = jnp.exp(jnp.concatenate([z[:, :, :1], z[:, :, :-1]], axis=2) - z)
            p = jnp.exp(s - z)
            tfirst = lambda x: jnp.moveaxis(x, 2, 0)
            qT, kT, vT, pT, gT = map(tfirst, (q * scale, k, v, p, g))
            b, h = (q.shape[0], q.shape[1])
            hk0 = jnp.zeros((b, h, q.shape[-1], s.shape[-1]), q.dtype)

            def step_k(hk, x):
                q_t, k_t, p_t, g_t = x
                hk = hk * g_t[:, :, None, :] + k_t[..., None] * p_t[:, :, None, :]
                return (hk, jnp.einsum('bhk,bhkm->bhm', q_t, hk))
            _, okT = jax.lax.scan(step_k, hk0, (qT, kT, pT, gT))
            pvT = jax.nn.softmax(okT, axis=-1)
            hv0 = jnp.zeros((b, h, s.shape[-1], v.shape[-1]), q.dtype)

            def step_v(hv, x):
                pv_t, v_t, p_t, g_t = x
                hv = hv * g_t[..., None] + p_t[..., None] * v_t[:, :, None, :]
                return (hv, jnp.einsum('bhm,bhmv->bhv', pv_t, hv))
            _, ovT = jax.lax.scan(step_v, hv0, (pvT, vT, pT, gT))
            return jnp.moveaxis(ovT, 0, 2)
        b, t, _ = hidden_states.shape
        to_heads = lambda x, d: jnp.transpose(x.reshape(b, t, H, d), (0, 2, 1, 3))
        q = to_heads(hidden_states @ Wq, DK)
        k = to_heads(hidden_states @ Wk, DK)
        v = to_heads(hidden_states @ Wv, DV)
        s = jnp.clip(to_heads(hidden_states @ Ws, M), CLAMP_MIN, CLAMP_MAX)
        o = jnp.transpose(_chunk_abc(q, k, v, s), (0, 2, 1, 3))
        g = (hidden_states @ Wg).reshape(b, t, H, DV)
        o = o * jax.lax.rsqrt(jnp.mean(jnp.square(o), axis=-1, keepdims=True) + EPS) * g_norm_weight
        o = o * (g * jax.nn.sigmoid(g))
        return o.reshape(b, t, VALUE_DIM) @ Wo

    def _L0_ffn_ref(x, W1, W2, W3):
        import jax, jax.numpy as jnp
        import numpy as np
        B, S, D, H = (4, 512, 512, 2048)

        def fwht(x):
            orig_shape = x.shape
            n = orig_shape[-1]
            x = x.reshape(-1, n)
            h = 1
            while h < n:
                xb = x.reshape(-1, n // (2 * h), 2, h)
                a = xb[:, :, 0, :]
                b = xb[:, :, 1, :]
                x = jnp.stack([a + b, a - b], axis=2).reshape(-1, n)
                h *= 2
            scale = jnp.asarray(1.0 / np.sqrt(n), dtype=x.dtype)
            return (x * scale).reshape(orig_shape)
        up_gate = jnp.einsum('bsd,hd->bsh', x, W1)
        up_lin = jnp.einsum('bsd,hd->bsh', x, W3)
        hidden = jax.nn.silu(up_gate) * up_lin
        hidden = fwht(hidden)
        out = jnp.einsum('bsh,dh->bsd', hidden, W2)
        return out
    x = L0_attn_hidden_states
    x = _layernorm(x + _L0_attn_ref(x, L0_attn_Wq, L0_attn_Wk, L0_attn_Wv, L0_attn_Wg, L0_attn_Ws, L0_attn_Wo, L0_attn_g_norm_weight), axis=-1)
    x = _layernorm(x + _L0_ffn_ref(x, L0_ffn_W1, L0_ffn_W2, L0_ffn_W3), axis=-1)
    return x

_drawn_inputs = setup_inputs


def setup_inputs(seed=0):
    import zlib

    import numpy as np

    out = dict(_drawn_inputs(seed))
    spreads = {'L0_attn_g_norm_weight': (1.0, 0.6)}
    factors = {'L0_attn_Wq': 8.0,
     'L0_attn_Wk': 8.0,
     'L0_attn_Wv': 5.125,
     'L0_attn_Wg': 5.15,
     'L0_attn_Ws': 8.0,
     'L0_attn_Wo': 5.149}
    for name, (base, spread) in spreads.items():
        noise = np.random.default_rng([zlib.crc32(name.encode()), seed]).standard_normal(out[name].shape)
        drawn = base * np.exp(spread * noise) if base else spread * noise
        out[name] = jnp.asarray(drawn.astype(out[name].dtype))
    for name, factor in factors.items():
        out[name] = (out[name] * factor).astype(out[name].dtype)
    return out
```

```python
from contextlib import ExitStack

import numpy as np

import concourse.bass as bass
from concourse import mybir

ALU = mybir.AluOpType
ACT = mybir.ActivationFunctionType
AX_X = mybir.AxisListType.X
F32 = mybir.dt.float32
F32R = mybir.dt.float32r

P = 128
B, T, D = 2, 2048, 512
H, DK, DV, M = 16, 64, 128, 64
FF = 2048
EPS = 1e-5
CLAMP = 32.0
KT = D // P

HG = 4
NG = H // HG
PAIRS = HG // 2
ST = 2 * P
NB = T // ST
NCH = B * T // P
NST = B * T // ST
QC, KC, SC, VC, GC = 0, HG * DK, 2 * HG * DK, 2 * HG * DK + HG * M, 2 * HG * DK + HG * M + HG * DV
WC = GC + HG * DV
WTILES = KT * WC // 512
OTILES = HG
STAGED = WTILES + OTILES + 2 * NST

HT = 4
NHG = FF // (HT * P)
TT = 4
NFS = B * T // (TT * P)
NTILE = B * T // P
RING = 4
ONE = 1
FSTAGED = 3 * HT + TT


def split_product(pe, out, terms):
    last = None
    for n, ((a_hi, a_lo), (b_hi, b_lo)) in enumerate(terms):
        pe.matmul(out, a_hi, b_hi, start=(n == 0), stop=False)
        pe.matmul(out, a_hi, b_lo, start=False, stop=False)
        last = pe.matmul(out, a_lo, b_hi, start=False, stop=(n == len(terms) - 1))
    return last


NEWTON = 1 + 3 * 3


def rsqrt(dve, x, y, a, step, base):
    dve.tensor_scalar(y.bitcast(mybir.dt.int32), x.bitcast(mybir.dt.int32), -0.5, float(0x5F375A86),
                      ALU.mult, ALU.add).then_inc(step, 1)
    for k in range(3):
        dve.wait_ge(step, base + (3 * k + 1))
        dve.tensor_tensor(a, y, y, ALU.mult).then_inc(step, 1)
        dve.wait_ge(step, base + (3 * k + 2))
        dve.scalar_tensor_tensor(out=a, in0=a, scalar=-0.5, in1=x, op0=ALU.mult, op1=ALU.mult).then_inc(step, 1)
        dve.wait_ge(step, base + (3 * k + 3))
        dve.scalar_tensor_tensor(out=y, in0=a, scalar=1.5, in1=y, op0=ALU.add, op1=ALU.mult).then_inc(step, 1)


def hadamard_of_w2(nc, consts, w2t, w2f):
    A = FF // P
    scale = float(np.float32(1.0 / np.sqrt(FF))) * 0.5
    NS = 4
    STEPS = (1, 2, 4, 8)
    with ExitStack() as ctx:
        sb = lambda n, s, d=F32: ctx.enter_context(nc.sbuf_tensor(n, s, d))
        sem = lambda n: ctx.enter_context(nc.semaphore(n))
        had = sb("had", [P, P])
        fly = [[sb(f"fly{s}_{j}", [P, A, P]) for j in range(2)] for s in range(2)]
        res = [sb(f"w2res{s}", [P, A, P]) for s in range(2)]
        bank = [ctx.enter_context(nc.psum_tensor(f"hbank{j}", [P, 4, P], F32)) for j in range(4)]
        had_in = sem("had_in")
        slice_in = [sem(f"slice_in{j}") for j in range(2)]
        fly_done = sem("fly_done")
        had_done = sem("had_done")
        scaled = sem("scaled")
        stored = [sem(f"w2_stored{j}") for j in range(2)]
        block = ctx.enter_context(nc.Block())

        @block.sync
        def _(sp):
            sp.dma_start(had[:, :], consts[:, 2 * P:3 * P]).then_inc(had_in, 16)
            for s in range(NS):
                if s >= 2:
                    sp.wait_ge(had_done, 4 * (s - 1))
                sp.dma_start(fly[s % 2][0][:, :, :], w2t[s]).then_inc(slice_in[s % 2], 16)
            for s in range(NS):
                sp.wait_ge(scaled, 4 * (s + 1))
                sp.dma_start(w2f[:, :, s * P:(s + 1) * P].rearrange("a p d -> p a d"),
                             res[s % 2][:, :, :]).then_inc(stored[s % 2], 16)
            for j in range(2):
                sp.wait_ge(stored[j], 16 * NS // 2)

        @block.vector
        def _(dve):
            n = 0
            for s in range(NS):
                dve.wait_ge(slice_in[s % 2], 16 * (s // 2 + 1))
                for j, h in enumerate(STEPS):
                    if j:
                        dve.wait_ge(fly_done, n)
                    src = fly[s % 2][j % 2][:, :, :].rearrange("p (n t h) d -> p n t h d", t=2, h=h)
                    dst = fly[s % 2][1 - j % 2][:, :, :].rearrange("p (n t h) d -> p n t h d", t=2, h=h)
                    for k in range(A // (2 * h)):
                        a, b = src[:, k, 0], src[:, k, 1]
                        dve.tensor_tensor(dst[:, k, 0], a, b, ALU.add).then_inc(fly_done, 1)
                        dve.tensor_tensor(dst[:, k, 1], a, b, ALU.subtract).then_inc(fly_done, 1)
                        n += 2

        @block.tensor
        def _(pe):
            pe.wait_ge(had_in, 16)
            per = sum(A // h for h in STEPS)
            for s in range(NS):
                pe.wait_ge(fly_done, per * (s + 1))
                for j in range(4):
                    if s:
                        pe.wait_ge(scaled, 4 * (s - 1) + j + 1)
                    pe.matmul(bank[j][:, :, :], had[:, :], fly[s % 2][0][:, 4 * j:4 * j + 4, :],
                              start=True, stop=True).then_inc(had_done, 1)

        @block.scalar
        def _(act):
            for s in range(NS):
                if s >= 2:
                    act.wait_ge(stored[s % 2], 16 * (s // 2))
                for j in range(4):
                    act.wait_ge(had_done, 4 * s + j + 1)
                    act.activation(res[s % 2][:, 4 * j:4 * j + 4, :], bank[j][:, :, :], ACT.Copy,
                                   scale=scale).then_inc(scaled, 1)


def attention(nc, consts, x_tok, xt, wt, wo, gw, yacc):
    with ExitStack() as ctx:
        sb = lambda n, s, d=F32: ctx.enter_context(nc.sbuf_tensor(n, s, d))
        ps = lambda n, s: ctx.enter_context(nc.psum_tensor(n, s, F32))
        sem = lambda n: ctx.enter_context(nc.semaphore(n))

        cst = sb("cst", [P, 2, P])
        ident, causal = cst[:, 0, :], cst[:, 1, :]
        gwc = sb("gwc", [P, 1])
        w_hi, w_lo = sb("w_hi", [P, KT, WC], F32R), sb("w_lo", [P, KT, WC], F32R)
        wo_hi, wo_lo = sb("wo_hi", [P, HG, D], F32R), sb("wo_lo", [P, HG, D], F32R)
        w_hi_flat = w_hi[:, :, :].rearrange("p k c -> p (k c)")
        w_lo_flat = w_lo[:, :, :].rearrange("p k c -> p (k c)")
        stage = [sb(f"stage{j}", [P, 512]) for j in range(2)]
        x_hi = [sb(f"x_hi{b}", [P, KT, ST], F32R) for b in range(B)]
        x_lo = [sb(f"x_lo{b}", [P, KT, ST], F32R) for b in range(B)]
        qT = [sb(f"qT{b}", [P, PAIRS, ST]) for b in range(B)]
        kT = [sb(f"kT{b}", [P, PAIRS, ST]) for b in range(B)]
        eT = [sb(f"eT{b}", [P, PAIRS, ST]) for b in range(B)]
        zT = [sb(f"zT{b}", [P, PAIRS, ST]) for b in range(B)]
        carry = [sb(f"carry{b}", [P, PAIRS]) for b in range(B)]
        ke = sb("ke", [P, 2, PAIRS, P])
        k_tok, e_tok = ke[:, 0], ke[:, 1]
        rz = sb("rz", [P, HG, M])
        v_tok = sb("v_tok", [P, HG, DV])
        gate = sb("gate", [P, HG * DV])
        qk = sb("qk", [P, 2, PAIRS, P])
        ep = sb("ep", [P, 2, PAIRS, P])
        sm = sb("sm", [P, HG, M])
        pv = sb("pv", [P, HG, M])
        pvT = sb("pvT", [P, PAIRS, P])
        hk = [sb(f"hk{b}", [P, PAIRS, 2 * M]) for b in range(B)]
        hv = [sb(f"hv{b}", [P, PAIRS, 2 * DV]) for b in range(B)]
        ow = sb("ow", [P, HG, DV])
        oT_hi, oT_lo = sb("oT_hi", [P, HG * P], F32R), sb("oT_lo", [P, HG * P], F32R)
        row_max, row_sum, row_rcp = sb("row_max", [P, HG]), sb("row_sum", [P, HG]), sb("row_rcp", [P, HG])
        ssq, t1, t2, t3, fac = (sb(n, [P, HG]) for n in ("ssq", "t1", "t2", "t3", "fac"))

        bk_v = ps("bk_v", [P, 512])
        bk_g = ps("bk_g", [P, 512])
        bk_ab = [ps(f"bk_ab{e}", [P, 2, PAIRS, P]) for e in range(2)]
        bk_ok = ps("bk_ok", [P, 512])
        bk_ov = ps("bk_ov", [P, HG, DV])
        bk_t = ps("bk_t", [P, 512])
        bk_u = ps("bk_u", [P, 512])

        cst_in, x_in = sem("cst_in"), sem("x_in")
        staged = [sem(f"staged{j}") for j in range(2)]
        st_hi, st_lo = sem("st_hi"), sem("st_lo")
        s_done, q_done, k_done = sem("s_done"), sem("q_done"), sem("k_done")
        clipped, e_ready, scanned, z_ready = sem("clipped"), sem("e_ready"), sem("scanned"), sem("z_ready")
        carried = sem("carried")
        q_ready, k_ready = sem("q_ready"), sem("k_ready")
        ke_done, ke_ready = sem("ke_done"), sem("ke_ready")
        qk_done, qk_ready = sem("qk_done"), sem("qk_ready")
        rz_done, rz_ready = sem("rz_done"), sem("rz_ready")
        v_done, v_ready = sem("v_done"), sem("v_ready")
        ok_done, okz_ready, max_ready, sub_ready = sem("ok_done"), sem("okz_ready"), sem("max_ready"), sem("sub_ready")
        exp_ready, sum_ready, pv_ready = sem("exp_ready"), sem("sum_ready"), sem("pv_ready")
        rcp_ready = sem("rcp_ready")
        hk_done, hk_ready = sem("hk_done"), sem("hk_ready")
        g_done, tanh_ready, gate_ready = sem("g_done"), sem("tanh_ready"), sem("gate_ready")
        pvT_done, pvT_ready = sem("pvT_done"), sem("pvT_ready")
        ep_done, ep_ready = sem("ep_done"), sem("ep_ready")
        ov_done, sq_ready, ssq_ready = sem("ov_done"), sem("sq_ready"), sem("ssq_ready")
        t1_ready, t2_ready, t3_ready, fac_ready = sem("t1_ready"), sem("t2_ready"), sem("t3_ready"), sem("fac_ready")
        ow_ready = sem("ow_ready")
        hv_done, hv_ready = sem("hv_done"), sem("hv_ready")
        oT_done, oT_hi_ready, oT_lo_ready = sem("oT_done"), sem("oT_hi_ready"), sem("oT_lo_ready")
        y_done, y_added = sem("y_done"), sem("y_added")
        zeroed, newton = sem("zeroed"), sem("newton")

        def steps(eng, one_step):
            one_step(0)
            with eng.Fori(1, NB - 1) as i:
                one_step(i)
            one_step(NB - 1)

        def chunk(g, i, r):
            return NCH * g + 4 * i + (r + 1)

        def super_(g, i, b):
            return NST * g + 2 * i + (b + 1)

        def tile_x(g, i, b, half):
            return STAGED * g + 4 * i + (WTILES + OTILES + 2 * b + half + 1)

        block = ctx.enter_context(nc.Block())

        @block.sync
        def _(sp):
            sp.dma_start(cst[:, :, :], consts[:, 0:2 * P].rearrange("p (a c) -> p a c", a=2)).then_inc(cst_in, 16)
            sp.dma_start(gwc[:, :], gw).then_inc(cst_in, 16)
            with sp.Fori(0, NG) as g:
                for w in range(WTILES + OTILES):
                    sp.wait_ge(st_lo, ONE + STAGED * g + max(w - 1, 0))
                    src = wt[g, w] if w < WTILES else wo[g, w - WTILES]
                    sp.dma_start(stage[w % 2][:, :], src).then_inc(staged[w % 2], 16)
                with sp.Fori(0, NB) as i:
                    for b in range(B):
                        for half in range(2):
                            sp.wait_ge(st_lo, ONE + tile_x(g, i, b, half) - 2)
                            sp.dma_start(stage[half][:, :], xt[b, i, half]).then_inc(staged[half], 16)

        @block.gpsimd
        def _(pool):
            for c in range(4):
                pool.dma_start(yacc[:, 8 * c:8 * c + 8, :], x_tok[:, 8 * c:8 * c + 8, :]).then_inc(x_in, 16)

            def x_low(g, i, b):
                for half in range(2):
                    pool.wait_ge(st_hi, tile_x(g, i, b, half))
                    dst = slice(half * 2, half * 2 + 2)
                    pool.tensor_tensor(x_lo[b][:, dst, :].rearrange("p k t -> p (k t)"), stage[half][:, :],
                                       x_hi[b][:, dst, :].rearrange("p k t -> p (k t)"), ALU.subtract)\
                        .then_inc(st_lo, 1)

            with pool.Fori(0, NG) as g:
                pool.wait_ge(st_lo, ONE + STAGED * g + (WTILES + OTILES))
                x_low(g, 0, 0)

                def one_step(i):
                    x_low(g, i, 1)
                    if not (isinstance(i, int) and i == NB - 1):
                        x_low(g, i + 1, 0)

                steps(pool, one_step)

        @block.scalar
        def _(act):
            act.wait_ge(cst_in, 32)

            def x_high(g, i, b):
                for half in range(2):
                    act.wait_ge(staged[half], (STAGED // 2 * g + 2 * i + (WTILES + OTILES) // 2 + b + 1) * 16)
                    act.activation(x_hi[b][:, half * 2:half * 2 + 2, :].rearrange("p k t -> p (k t)"),
                                   stage[half][:, :], ACT.Copy).then_inc(st_hi, 1)

            def exp_s(g, i, b):
                act.wait_ge(clipped, super_(g, i, b))
                act.activation(eT[b][:, :, :], eT[b][:, :, :], ACT.Exp).then_inc(e_ready, 1)

            def q_copy(g, i, b):
                act.wait_ge(q_done, super_(g, i, b))
                act.activation(qT[b][:, :, :], bk_g[:, :].rearrange("p (a t) -> p a t", a=PAIRS), ACT.Copy)\
                    .then_inc(q_ready, 1)

            def k_copy(g, i, b):
                act.wait_ge(k_done, super_(g, i, b))
                act.activation(kT[b][:, :, :], bk_v[:, :].rearrange("p (a t) -> p a t", a=PAIRS), ACT.Copy)\
                    .then_inc(k_ready, 1)

            def square_o(g, i, r):
                act.wait_ge(ov_done, chunk(g, i, r))
                act.activation(ow[:, :, :], bk_ov[:, :, :], ACT.Square).then_inc(sq_ready, 1)

            def o_high(g, i, r):
                act.wait_ge(oT_done, chunk(g, i, r))
                act.activation(oT_hi[:, :], bk_t[:, :], ACT.Copy).then_inc(oT_hi_ready, 1)

            with act.Fori(0, NG) as g:
                for w in range(WTILES + OTILES):
                    act.wait_ge(staged[w % 2], (STAGED // 2 * g + (w // 2 + 1)) * 16)
                    if w == 0:
                        act.wait_ge(g_done, ONE + NCH * g)
                    if w < WTILES:
                        act.activation(w_hi_flat[:, 512 * w:512 * w + 512], stage[w % 2][:, :], ACT.Copy)\
                            .then_inc(st_hi, 1)
                    else:
                        if w == WTILES:
                            act.wait_ge(y_done, ONE + NCH * g)
                        act.activation(wo_hi[:, w - WTILES, :], stage[w % 2][:, :], ACT.Copy,
                                       scale=gwc[:, 0:1]).then_inc(st_hi, 1)
                x_high(g, 0, 0)
                exp_s(g, 0, 0)
                q_copy(g, 0, 0)
                k_copy(g, 0, 0)

                def one_step(i):
                    start = isinstance(i, int) and i == 0
                    end = isinstance(i, int) and i == NB - 1
                    for r in range(4):
                        b = r // 2
                        n = chunk(g, i, r)
                        nxt = (i, 1) if r < 2 else (i + 1, 0)
                        if not (start and r < 2):
                            o_high(g, i, r - 2)
                        if not (start and r == 0):
                            square_o(g, i, r - 1)
                        if r % 2 == 0 and not (end and r == 2):
                            act.wait_ge(g_done, ONE + n - 1)
                            x_high(g, *nxt)
                        act.wait_ge(ke_done, n)
                        act.activation(ke[:, :, :, :], bk_t[:, :].rearrange("p (a c t) -> p a c t", a=2, c=2),
                                       ACT.Copy).then_inc(ke_ready, 1)
                        act.wait_ge(rz_done, n)
                        act.activation(rz[:, :, :], bk_u[:, 0:HG * M].rearrange("p (h m) -> p h m", h=HG),
                                       ACT.Copy).then_inc(rz_ready, 1)
                        act.wait_ge(v_done, n)
                        act.activation(v_tok[:, :, :], bk_v[:, :].rearrange("p (h v) -> p h v", h=HG),
                                       ACT.Copy).then_inc(v_ready, 1)
                        act.wait_ge(sub_ready, n)
                        act.activation(sm[:, :, :], sm[:, :, :], ACT.Exp, scale=DK ** -0.5).then_inc(exp_ready, 1)
                        act.wait_ge(g_done, ONE + n)
                        act.wait_ge(ow_ready, ONE + HG * (n - 1))
                        act.activation(gate[:, :], bk_g[:, :], ACT.Tanh, scale=0.5).then_inc(tanh_ready, 1)
                        act.wait_ge(pvT_done, n)
                        act.activation(pvT[:, :, :], bk_ok[:, 256:512].rearrange("p (a t) -> p a t", a=PAIRS),
                                       ACT.Copy).then_inc(pvT_ready, 1)
                        if not (end and r >= 2):
                            if r % 2 == 0:
                                exp_s(g, *nxt)
                            else:
                                q_copy(g, *nxt)
                                k_copy(g, *nxt)

                steps(act, one_step)
                o_high(g, NB - 1, 2)
                square_o(g, NB - 1, 3)
                o_high(g, NB - 1, 3)

        @block.vector
        def _(dve):
            dve.wait_ge(cst_in, 32)
            dve.wait_ge(x_in, 64)

            def clip_s(g, i, b):
                dve.wait_ge(s_done, super_(g, i, b))
                dve.tensor_scalar(eT[b][:, :, :], bk_g[:, :].rearrange("p (a t) -> p a t", a=PAIRS),
                                  CLAMP, -CLAMP, ALU.min, ALU.max).then_inc(clipped, 1)

            def scan_e(g, i, b):
                dve.wait_ge(e_ready, super_(g, i, b))
                for a in range(PAIRS):
                    dve.tensor_tensor_scan(zT[b][:, a, :], eT[b][:, a, :], eT[b][:, a, :], carry[b][:, a:a + 1],
                                           ALU.add, ALU.max).then_inc(scanned, 1)
                dve.wait_ge(scanned, 2 * super_(g, i, b))
                dve.tensor_copy(carry[b][:, :], zT[b][:, :, ST - 1]).then_inc(carried, 1)

            def invert_z(g, i, b):
                dve.wait_ge(carried, super_(g, i, b))
                dve.reciprocal(zT[b][:, :, :], zT[b][:, :, :]).then_inc(z_ready, 1)

            def update_hv(g, i, r):
                b = r % 4 // 2
                dve.wait_ge(hv_done, chunk(g, i, r))
                upd = bk_u[:, :].rearrange("p (a c) -> p a c", a=PAIRS)
                for e in range(2):
                    rows, cols = slice(64 * e, 64 * e + 64), slice(DV * e, DV * e + DV)
                    dve.tensor_tensor(hv[b][rows, :, cols], hv[b][rows, :, cols], upd[rows, :, cols], ALU.add)\
                        .then_inc(hv_ready, 1)

            def update_hk(g, i, r):
                b = r // 2
                dve.wait_ge(hk_done, chunk(g, i, r))
                upd = bk_u[:, 256:512].rearrange("p (a c) -> p a c", a=PAIRS)
                for e in range(2):
                    rows, cols = slice(64 * e, 64 * e + 64), slice(M * e, M * e + M)
                    dve.tensor_tensor(hk[b][rows, :, cols], hk[b][rows, :, cols], upd[rows, :, cols], ALU.add)\
                        .then_inc(hk_ready, 1)

            def factor_o(g, i, r):
                n = chunk(g, i, r)
                dve.wait_ge(sq_ready, n)
                dve.tensor_reduce(ssq[:, :], ow[:, :, :], AX_X, ALU.add).then_inc(ssq_ready, 1)
                dve.wait_ge(ssq_ready, n)
                dve.wait_ge(rcp_ready, n)
                dve.tensor_tensor(t1[:, :], ssq[:, :], row_rcp[:, :], ALU.mult).then_inc(t1_ready, 1)
                dve.wait_ge(t1_ready, n)
                dve.tensor_tensor(t2[:, :], t1[:, :], row_rcp[:, :], ALU.mult).then_inc(t2_ready, 1)
                dve.wait_ge(t2_ready, n)
                dve.tensor_scalar(t1[:, :], t2[:, :], 1.0, DV * EPS, ALU.mult, ALU.add).then_inc(t3_ready, 1)
                dve.wait_ge(t3_ready, n)
                rsqrt(dve, t1[:, :], t3[:, :], t2[:, :], newton, NEWTON * (n - 1))
                dve.wait_ge(newton, NEWTON * n)
                dve.scalar_tensor_tensor(out=fac[:, :], in0=t3[:, :], scalar=0.5 * DV ** 0.5, in1=row_rcp[:, :],
                                         op0=ALU.mult, op1=ALU.mult).then_inc(fac_ready, 1)

            def gate_o(g, i, r):
                n = chunk(g, i, r)
                dve.wait_ge(fac_ready, n)
                dve.wait_ge(gate_ready, ONE + n)
                for h in range(HG):
                    dve.scalar_tensor_tensor(out=ow[:, h, :], in0=bk_ov[:, h, :], scalar=fac[:, h:h + 1],
                                             in1=gate[:, h * DV:(h + 1) * DV], op0=ALU.mult, op1=ALU.mult)\
                        .then_inc(ow_ready, 1)

            def o_low(g, i, r):
                dve.wait_ge(oT_hi_ready, chunk(g, i, r))
                dve.tensor_tensor(oT_lo[:, :], bk_t[:, :], oT_hi[:, :], ALU.subtract).then_inc(oT_lo_ready, 1)

            def add_y(g, i, r):
                at = T // P * (r % 4 // 2) + 2 * i + r % 2 - 2 * (r < 0)
                dve.wait_ge(y_done, ONE + chunk(g, i, r))
                dve.tensor_tensor(yacc[:, at, :], yacc[:, at, :], bk_v[:, :], ALU.add).then_inc(y_added, 1)

            with dve.Fori(0, NG) as g:
                for w in range(WTILES + OTILES):
                    dve.wait_ge(st_hi, STAGED * g + w + 1)
                    if w < WTILES:
                        part = slice(512 * w, 512 * w + 512)
                        dve.tensor_tensor(w_lo_flat[:, part], stage[w % 2][:, :], w_hi_flat[:, part],
                                          ALU.subtract).then_inc(st_lo, 1)
                    else:
                        dve.scalar_tensor_tensor(out=wo_lo[:, w - WTILES, :], in0=stage[w % 2][:, :],
                                                 scalar=gwc[:, 0:1], in1=wo_hi[:, w - WTILES, :],
                                                 op0=ALU.mult, op1=ALU.subtract).then_inc(st_lo, 1)
                for b in range(B):
                    for t in (hk[b], hv[b]):
                        dve.memset(t[:, :, :], 0.0).then_inc(zeroed, 1)
                    dve.memset(carry[b][:, :], 0.0).then_inc(zeroed, 1)
                dve.wait_ge(zeroed, 6 * g + 6)
                clip_s(g, 0, 0)
                scan_e(g, 0, 0)
                invert_z(g, 0, 0)

                def one_step(i):
                    start = isinstance(i, int) and i == 0
                    end = isinstance(i, int) and i == NB - 1
                    for r in range(4):
                        b = r // 2
                        n = chunk(g, i, r)
                        nxt = (i, 1) if r < 2 else (i + 1, 0)
                        first = start and r == 0
                        more = not (end and r >= 2)
                        behind = start and r < 2
                        if not behind:
                            o_low(g, i, r - 2)
                        if not first:
                            update_hv(g, i, r - 1)
                        dve.wait_ge(qk_done, n)
                        mask = causal.unsqueeze(1).broadcast_to([P, PAIRS, P])
                        for e in range(2):
                            dve.tensor_tensor(qk[:, e], bk_ab[e][:, 0], mask, ALU.mult).then_inc(qk_ready, 1)
                        if not first:
                            factor_o(g, i, r - 1)
                        if r % 2 == 1 and more:
                            scan_e(g, *nxt)
                        dve.wait_ge(ok_done, n)
                        dve.wait_ge(rz_ready, n)
                        dve.tensor_tensor(sm[:, :, :], bk_ok[:, 0:HG * M].rearrange("p (h m) -> p h m", h=HG),
                                          rz[:, :, :], ALU.mult).then_inc(okz_ready, 1)
                        dve.wait_ge(okz_ready, n)
                        dve.tensor_reduce(row_max[:, :], sm[:, :, :], AX_X, ALU.max).then_inc(max_ready, 1)
                        dve.wait_ge(max_ready, n)
                        dve.tensor_tensor(sm[:, :, :], sm[:, :, :], row_max[:, :].unsqueeze(2).broadcast_to([P, HG, M]),
                                          ALU.subtract).then_inc(sub_ready, 1)
                        if not first:
                            gate_o(g, i, r - 1)
                        update_hk(g, i, r)
                        dve.wait_ge(exp_ready, n)
                        dve.tensor_tensor(pv[:, :, :], sm[:, :, :], rz[:, :, :], ALU.mult).then_inc(pv_ready, 1)
                        dve.tensor_reduce(row_sum[:, :], sm[:, :, :], AX_X, ALU.add).then_inc(sum_ready, 1)
                        dve.wait_ge(sum_ready, n)
                        dve.reciprocal(row_rcp[:, :], row_sum[:, :]).then_inc(rcp_ready, 1)
                        dve.wait_ge(tanh_ready, n)
                        dve.scalar_tensor_tensor(out=gate[:, :], in0=gate[:, :], scalar=1.0, in1=bk_g[:, :],
                                                 op0=ALU.add, op1=ALU.mult).then_inc(gate_ready, 1)
                        if not behind:
                            add_y(g, i, r - 2)
                        if r % 2 == 1 and more:
                            invert_z(g, *nxt)
                        dve.wait_ge(ep_done, n)
                        for e in range(2):
                            dve.tensor_tensor(ep[:, e], bk_ab[e][:, 1], mask, ALU.mult).then_inc(ep_ready, 1)
                        if r % 2 == 0 and more:
                            clip_s(g, *nxt)

                steps(dve, one_step)
                o_low(g, NB - 1, 2)
                update_hv(g, NB - 1, 3)
                factor_o(g, NB - 1, 3)
                gate_o(g, NB - 1, 3)
                add_y(g, NB - 1, 2)
                o_low(g, NB - 1, 3)
                add_y(g, NB - 1, 3)

        @block.tensor
        def _(pe):
            for started in (st_lo, g_done, y_done, gate_ready, y_added, oT_lo_ready, ep_ready, hv_ready, hk_ready,
                            pvT_ready, ow_ready):
                pe.sem_inc(started, ONE)
            pe.wait_ge(cst_in, 32)

            def transposed(out, b, col, a):
                c = slice(col + a * P, col + a * P + P)
                return split_product(pe, out[:, a * ST:(a + 1) * ST],
                                     [((w_hi[:, k, c], w_lo[:, k, c]), (x_hi[b][:, k, :], x_lo[b][:, k, :]))
                                      for k in range(KT)])

            def by_token(out, b, half, col):
                t = slice(half * P, half * P + P)
                c = slice(col, col + 512)
                return split_product(pe, out[:, :],
                                     [((x_hi[b][:, k, t], x_lo[b][:, k, t]), (w_hi[:, k, c], w_lo[:, k, c]))
                                      for k in range(KT)])

            def values(g, i, r):
                b = r % 4 // 2
                n = chunk(g, i, r)
                pe.wait_ge(ep_ready, ONE + 2 * n)
                pe.wait_ge(hv_ready, ONE + 2 * n - 2)
                pe.wait_ge(ow_ready, ONE + 4 * n - 4)
                pe.wait_ge(v_ready, n)
                for a in range(PAIRS):
                    pe.matmul(bk_ov[:, 2 * a:2 * a + 2, :], pvT[:, a, :], hv[b][:, a, :].rearrange("p (e v) -> p e v", e=2),
                              start=True, stop=False)
                    for e in range(2):
                        mm = pe.matmul(bk_ov[:, 2 * a + e, :], ep[:, e, a, :], v_tok[:, 2 * a + e, :],
                                       start=False, stop=(e == 1))
                mm.then_inc(ov_done, 1)
                pe.wait_ge(hk_ready, ONE + 2 * n)
                for a in range(PAIRS):
                    mm = pe.matmul(bk_u[:, 256 * a:256 * a + 256], e_tok[:, a, :],
                                   v_tok[:, 2 * a:2 * a + 2, :].rearrange("p h v -> p (h v)"), start=True, stop=True)
                mm.then_inc(hv_done, 1)

            def turn_o(g, i, r):
                n = chunk(g, i, r)
                pe.wait_ge(ow_ready, ONE + 4 * n)
                for h in range(HG):
                    mm = pe.transpose(bk_t[:, P * h:P * h + P], ow[:, h, :], ident)
                mm.then_inc(oT_done, 1)

            def project_y(g, i, r):
                pe.wait_ge(oT_lo_ready, ONE + chunk(g, i, r))
                split_product(pe, bk_v[:, :], [((oT_hi[:, P * h:P * h + P], oT_lo[:, P * h:P * h + P]),
                                                (wo_hi[:, h, :], wo_lo[:, h, :])) for h in range(HG)])\
                    .then_inc(y_done, 1)

            with pe.Fori(0, NG) as g:
                pe.wait_ge(zeroed, 6 * g + 6)
                pe.wait_ge(st_lo, ONE + tile_x(g, 0, 0, 1))
                pe.wait_ge(gate_ready, ONE + NCH * g)
                for a in range(PAIRS):
                    mm = transposed(bk_g, 0, SC, a)
                mm.then_inc(s_done, 1)
                pe.wait_ge(y_added, ONE + NCH * g)
                for a in range(PAIRS):
                    mm = transposed(bk_v, 0, KC, a)
                mm.then_inc(k_done, 1)
                pe.wait_ge(clipped, super_(g, 0, 0))
                for a in range(PAIRS):
                    mm = transposed(bk_g, 0, QC, a)
                mm.then_inc(q_done, 1)

                def one_step(i):
                    start = isinstance(i, int) and i == 0
                    end = isinstance(i, int) and i == NB - 1
                    for r in range(4):
                        b, half = r // 2, r % 2
                        n = chunk(g, i, r)
                        nxt = (i, 1) if r < 2 else (i + 1, 0)
                        nb = 1 - b
                        m = super_(g, *nxt)
                        first = start and r == 0
                        more = not (end and r >= 2)
                        t = slice(half * P, half * P + P)
                        behind = start and r < 2
                        if not behind:
                            pe.wait_ge(ke_ready, n - 1)
                            turn_o(g, i, r - 2)
                        if not first:
                            values(g, i, r - 1)
                        if half == 0:
                            pe.wait_ge(k_ready, super_(g, i, b))
                            pe.wait_ge(e_ready, super_(g, i, b))
                            pe.wait_ge(q_ready, super_(g, i, b))
                            pe.wait_ge(z_ready, super_(g, i, b))
                        if behind:
                            pe.wait_ge(oT_lo_ready, ONE + NCH * g)
                            if r == 1:
                                pe.wait_ge(ke_ready, n - 1)
                        else:
                            pe.wait_ge(oT_lo_ready, ONE + n - 2)
                        for a in range(PAIRS):
                            pe.transpose(bk_t[:, P * a:P * a + P], kT[b][:, a, t], ident)
                        for a in range(PAIRS):
                            mm = pe.transpose(bk_t[:, 256 + P * a:256 + P * a + P], eT[b][:, a, t], ident)
                        mm.then_inc(ke_done, 1)
                        pe.wait_ge(ep_ready, ONE + 2 * n - 2)
                        for a in range(PAIRS):
                            for e in range(2):
                                rows = slice(64 * e, 64 * e + 64)
                                mm = pe.matmul(bk_ab[e][:, 0, a, :], kT[b][rows, a, t], qT[b][rows, a, t],
                                               start=True, stop=True)
                        mm.then_inc(qk_done, 1)
                        pe.wait_ge(hv_ready, ONE + 2 * n - 2)
                        for a in range(PAIRS):
                            mm = pe.transpose(bk_u[:, P * a:P * a + P], zT[b][:, a, t], ident)
                        mm.then_inc(rz_done, 1)
                        if half == 0:
                            pe.wait_ge(k_ready, super_(g, i, b))
                        elif behind:
                            pe.wait_ge(v_ready, n - 1)
                        else:
                            pe.wait_ge(y_added, ONE + n - 3)
                        by_token(bk_v, b, half, VC).then_inc(v_done, 1)
                        pe.wait_ge(qk_ready, 2 * n)
                        pe.wait_ge(ke_ready, n)
                        pe.wait_ge(hk_ready, ONE + 2 * n - 2)
                        pe.wait_ge(pvT_ready, ONE + n - 1)
                        for a in range(PAIRS):
                            pe.matmul(bk_ok[:, P * a:P * a + P], qT[b][:, a, t], hk[b][:, a, :], start=True, stop=False)
                            for e in range(2):
                                o = P * a + M * e
                                mm = pe.matmul(bk_ok[:, o:o + M], qk[:, e, a, :], e_tok[:, a, M * e:M * e + M],
                                               start=False, stop=(e == 1))
                        mm.then_inc(ok_done, 1)
                        pe.wait_ge(rz_ready, n)
                        for a in range(PAIRS):
                            mm = pe.matmul(bk_u[:, 256 + P * a:256 + P * a + P], k_tok[:, a, :], e_tok[:, a, :],
                                           start=True, stop=True)
                        mm.then_inc(hk_done, 1)
                        if half == 0:
                            pe.wait_ge(q_ready, super_(g, i, b))
                        elif more:
                            pe.wait_ge(clipped, m)
                        else:
                            pe.wait_ge(gate_ready, ONE + n - 1)
                        by_token(bk_g, b, half, GC).then_inc(g_done, 1)
                        pe.wait_ge(v_ready, n)
                        if not behind:
                            project_y(g, i, r - 2)
                        pe.wait_ge(pv_ready, n)
                        for a in range(PAIRS):
                            mm = pe.transpose(bk_ok[:, 256 + P * a:256 + P * a + P],
                                              pv[:, 2 * a:2 * a + 2, :].rearrange("p h m -> p (h m)"), ident)
                        mm.then_inc(pvT_done, 1)
                        if more:
                            pe.wait_ge(gate_ready, ONE + n)
                            if half == 0:
                                pe.wait_ge(st_lo, ONE + tile_x(g, *nxt, 1))
                            transposed(bk_g, nb, SC if half == 0 else QC, 0)
                        pe.wait_ge(pvT_ready, ONE + n)
                        pe.wait_ge(qk_ready, 2 * n)
                        for a in range(PAIRS):
                            for e in range(2):
                                rows = slice(64 * e, 64 * e + 64)
                                mm = pe.matmul(bk_ab[e][:, 1, a, :], eT[b][rows, a, t], pvT[rows, a, :],
                                               start=True, stop=True)
                        mm.then_inc(ep_done, 1)
                        if more:
                            mm = transposed(bk_g, nb, SC if half == 0 else QC, 1)
                            mm.then_inc(s_done if half == 0 else q_done, 1)
                            if half == 1:
                                if not behind:
                                    pe.wait_ge(y_added, ONE + n - 2)
                                for a in range(PAIRS):
                                    mm = transposed(bk_v, nb, KC, a)
                                mm.then_inc(k_done, 1)

                steps(pe, one_step)
                pe.wait_ge(ke_ready, chunk(g, NB - 1, 3))
                turn_o(g, NB - 1, 2)
                values(g, NB - 1, 3)
                pe.wait_ge(y_added, ONE + chunk(g, NB - 1, 1))
                project_y(g, NB - 1, 2)
                pe.wait_ge(oT_lo_ready, ONE + chunk(g, NB - 1, 2))
                turn_o(g, NB - 1, 3)
                pe.wait_ge(y_added, ONE + chunk(g, NB - 1, 2))
                project_y(g, NB - 1, 3)


def layernorm(dve, yacc, stats, mv, rstd, spare, stat_ready, mv_ready, step, normed):
    with dve.Fori(0, NTILE) as n:
        dve.bn_stats(stats[:, n, :], yacc[:, n, :]).then_inc(stat_ready, 1)
    dve.wait_ge(stat_ready, NTILE)
    for n in range(NTILE):
        dve.bn_aggr(mv[:, n, :], stats[:, n, :]).then_inc(mv_ready, 1)
    dve.wait_ge(mv_ready, NTILE)
    dve.tensor_scalar(spare[:, 0, :], mv[:, :, 1], 1.0, EPS, ALU.mult, ALU.add).then_inc(step, 1)
    dve.wait_ge(step, 1)
    rsqrt(dve, spare[:, 0, :], rstd[:, :], spare[:, 1, :], step, 1)
    dve.wait_ge(step, 1 + NEWTON)
    for n in range(NTILE):
        dve.tensor_scalar(yacc[:, n, :], yacc[:, n, :], mv[:, n, 0:1], rstd[:, n:n + 1], ALU.subtract, ALU.mult)\
            .then_inc(normed, 1)


def norm_and_turn(nc, consts, yacc, x1t):
    with ExitStack() as ctx:
        sb = lambda n, s, d=F32: ctx.enter_context(nc.sbuf_tensor(n, s, d))
        sem = lambda n: ctx.enter_context(nc.semaphore(n))
        ident = sb("ident2", [P, P])
        stats, mv = sb("stats", [P, NTILE, 6]), sb("mv", [P, NTILE, 2])
        rstd, spare = sb("rstd", [P, NTILE]), sb("spare", [P, 2, NTILE])
        xt_out = [sb(f"xt_out{j}", [P, KT, TT * P]) for j in range(2)]
        bank = [ctx.enter_context(nc.psum_tensor(f"tbank{j}", [P, KT, P], F32)) for j in range(4)]
        id_in = sem("id_in")
        stat_ready, mv_ready, step, normed = sem("stat_ready"), sem("mv_ready"), sem("ln_step"), sem("normed")
        turned, copied = sem("turned"), sem("copied")
        stored = [sem(f"x1_stored{j}") for j in range(2)]
        block_left = sem("block_left")
        block = ctx.enter_context(nc.Block())
        assert TT == 4 and NFS % 2 == 0

        @block.sync
        def _(sp):
            sp.dma_start(ident[:, :], consts[:, 0:P]).then_inc(id_in, 16)
            with sp.Fori(0, NFS // 2) as s2:
                for j in range(2):
                    sp.wait_ge(copied, ONE + 2 * TT * s2 + TT * (j + 1))
                    for k in range(KT):
                        sp.dma_start(x1t[2 * s2 + j, k], xt_out[j][:, k, :]).then_inc(stored[j], 16)
                for j in range(2):
                    sp.wait_ge(stored[j], 16 * KT * s2 + 16 * KT)
                    sp.sem_inc(block_left, 1)

        @block.vector
        def _(dve):
            layernorm(dve, yacc, stats, mv, rstd, spare, stat_ready, mv_ready, step, normed)

        xn = [sb(f"xn{j}", [P, D]) for j in range(4)]
        xn_ready = sem("xn_ready")

        @block.gpsimd
        def _(pool):
            with pool.Fori(0, NFS) as s:
                for j in range(TT):
                    pool.wait_ge(normed, TT * s + (j + 1))
                    pool.wait_ge(turned, ONE + TT * s)
                    pool.tensor_copy(xn[j][:, :], yacc[:, TT * s + j, :]).then_inc(xn_ready, 1)

        @block.tensor
        def _(pe):
            for started in (turned, copied, block_left):
                pe.sem_inc(started, ONE)
            pe.wait_ge(id_in, 16)
            with pe.Fori(0, NFS) as s:
                for j in range(TT):
                    pe.wait_ge(xn_ready, TT * s + (j + 1))
                    pe.wait_ge(copied, ONE + TT * s)
                    for k in range(KT):
                        mm = pe.transpose(bank[j][:, k, :], xn[j][:, k * P:(k + 1) * P], ident[:, :])
                    mm.then_inc(turned, 1)

        @block.scalar
        def _(act):
            with act.Fori(0, NFS // 2) as s2:
                for half in range(2):
                    act.wait_ge(block_left, ONE + 2 * s2)
                    for j in range(TT):
                        act.wait_ge(turned, ONE + 2 * TT * s2 + (TT * half + j + 1))
                        act.activation(xt_out[half][:, :, j * P:(j + 1) * P], bank[j][:, :, :], ACT.Copy)\
                            .then_inc(copied, 1)


def feed_forward(nc, x1t, w13, w2f, yacc):
    with ExitStack() as ctx:
        sb = lambda n, s, d=F32: ctx.enter_context(nc.sbuf_tensor(n, s, d))
        ps = lambda n, s: ctx.enter_context(nc.psum_tensor(n, s, F32))
        sem = lambda n: ctx.enter_context(nc.semaphore(n))
        NW = 3 * HT
        w_hi, w_lo = sb("fw_hi", [P, NW, 512], F32R), sb("fw_lo", [P, NW, 512], F32R)
        stage = [sb(f"fstage{j}", [P, 512]) for j in range(RING)]
        x_hi, x_lo = sb("fx_hi", [P, KT, 512], F32R), sb("fx_lo", [P, KT, 512], F32R)
        th = [sb(f"th{j}", [P, 512]) for j in range(2)]
        hid = [sb(f"hid{j}", [P, 512]) for j in range(2)]
        h_hi, h_lo = sb("h_hi", [P, HT, 512], F32R), sb("h_lo", [P, HT, 512], F32R)
        bk_gate = [ps(f"bk_gate{j}", [P, 512]) for j in range(2)]
        bk_up = [ps(f"bk_up{j}", [P, 512]) for j in range(2)]
        bk_y = [ps(f"bk_y{j}", [P, 512]) for j in range(TT)]
        staged = [sem(f"fstaged{j}") for j in range(RING)]
        st_hi, st_lo = sem("fst_hi"), sem("fst_lo")
        gate_done, up_done, tanh_ready, act_ready, hid_ready = (sem(n) for n in (
            "fgate_done", "fup_done", "ftanh_ready", "fact_ready", "fhid_ready"))
        h_hi_ready, h_lo_ready = sem("h_hi_ready"), sem("h_lo_ready")
        y_done, y_added = sem("fy_done"), sem("fy_added")
        per = NW + KT * NFS
        assert NW % RING == 0 and KT == RING and HT == 4 and TT == 4

        block = ctx.enter_context(nc.Block())

        def hidden(g, s, h):
            return HT * NFS * g + HT * s + (h + 1)

        @block.sync
        def _(sp):
            with sp.Fori(0, NHG) as g:
                for w in range(NW):
                    sp.wait_ge(st_lo, ONE + per * g + max(w - RING + 1, 0))
                    src = w13[g, w] if w < 2 * KT else w2f[HT * g + (w - 2 * KT)]
                    sp.dma_start(stage[w % RING][:, :], src).then_inc(staged[w % RING], 16)
                with sp.Fori(0, NFS) as s:
                    for k in range(KT):
                        sp.wait_ge(st_lo, ONE + per * g + KT * s + (NW + k + 1 - RING))
                        sp.dma_start(stage[k][:, :], x1t[s, k]).then_inc(staged[k], 16)

        @block.scalar
        def _(act):
            def x_high(g, s):
                for k in range(KT):
                    act.wait_ge(staged[k], (per // RING * g + s + (NW // RING + 1)) * 16)
                    act.activation(x_hi[:, k, :], stage[k][:, :], ACT.Copy).then_inc(st_hi, 1)

            with act.Fori(0, NHG) as g:
                for w in range(NW):
                    act.wait_ge(staged[w % RING], (per // RING * g + (w // RING + 1)) * 16)
                    if w == 0:
                        act.wait_ge(y_done, ONE + TT * NFS * g)
                    act.activation(w_hi[:, w, :], stage[w % RING][:, :], ACT.Copy).then_inc(st_hi, 1)
                x_high(g, 0)

                def one_step(s):
                    for h in range(HT):
                        n = hidden(g, s, h)
                        act.wait_ge(gate_done, n)
                        act.activation(th[h % 2][:, :], bk_gate[h % 2][:, :], ACT.Tanh, scale=0.5)\
                            .then_inc(tanh_ready, 1)
                        act.wait_ge(hid_ready, ONE + n)
                        act.activation(h_hi[:, h, :], hid[h % 2][:, :], ACT.Copy).then_inc(h_hi_ready, 1)
                    if not isinstance(s, int):
                        x_high(g, s + 1)

                with act.Fori(0, NFS - 1) as s:
                    one_step(s)
                one_step(NFS - 1)

        @block.gpsimd
        def _(pool):
            def x_low(g, s):
                for k in range(KT):
                    pool.wait_ge(st_hi, per * g + KT * s + (NW + k + 1))
                    pool.tensor_tensor(x_lo[:, k, :], stage[k][:, :], x_hi[:, k, :], ALU.subtract).then_inc(st_lo, 1)

            with pool.Fori(0, NHG) as g:
                pool.wait_ge(st_lo, ONE + per * g + NW)
                x_low(g, 0)

                def one_step(s):
                    for h in range(HT):
                        n = hidden(g, s, h)
                        pool.wait_ge(h_hi_ready, n)
                        pool.tensor_tensor(h_lo[:, h, :], hid[h % 2][:, :], h_hi[:, h, :], ALU.subtract)\
                            .then_inc(h_lo_ready, 1)
                    if not isinstance(s, int):
                        x_low(g, s + 1)

                with pool.Fori(0, NFS - 1) as s:
                    one_step(s)
                one_step(NFS - 1)

        @block.vector
        def _(dve):
            with dve.Fori(0, NHG) as g:
                for w in range(NW):
                    dve.wait_ge(st_hi, per * g + (w + 1))
                    dve.tensor_tensor(w_lo[:, w, :], stage[w % RING][:, :], w_hi[:, w, :], ALU.subtract)\
                        .then_inc(st_lo, 1)
                with dve.Fori(0, NFS) as s:
                    for h in range(HT):
                        n = hidden(g, s, h)
                        dve.wait_ge(tanh_ready, n)
                        dve.scalar_tensor_tensor(out=th[h % 2][:, :], in0=th[h % 2][:, :], scalar=1.0,
                                                 in1=bk_gate[h % 2][:, :], op0=ALU.add, op1=ALU.mult)\
                            .then_inc(act_ready, 1)
                        dve.wait_ge(act_ready, n)
                        dve.wait_ge(up_done, n)
                        if h >= 2:
                            dve.wait_ge(h_lo_ready, ONE + n - 2)
                        else:
                            dve.wait_ge(h_lo_ready, ONE + HT * NFS * g + HT * s)
                        dve.tensor_tensor(hid[h % 2][:, :], th[h % 2][:, :], bk_up[h % 2][:, :], ALU.mult)\
                            .then_inc(hid_ready, 1)
                    for t in range(TT):
                        dve.wait_ge(y_done, ONE + TT * NFS * g + TT * s + (t + 1))
                        dve.tensor_tensor(yacc[:, TT * s + t, :], yacc[:, TT * s + t, :], bk_y[t][:, :], ALU.add)\
                            .then_inc(y_added, 1)

        @block.tensor
        def _(pe):
            for started in (st_lo, y_done, h_lo_ready, hid_ready, y_added):
                pe.sem_inc(started, ONE)
            with pe.Fori(0, NHG) as g:
                with pe.Fori(0, NFS) as s:
                    pe.wait_ge(st_lo, ONE + per * g + KT * s + (NW + KT))
                    for h in range(HT):
                        n = hidden(g, s, h)
                        c = slice(h * P, h * P + P)
                        if h >= 2:
                            pe.wait_ge(hid_ready, ONE + n - 2)
                        else:
                            pe.wait_ge(hid_ready, ONE + HT * NFS * g + HT * s)
                        for bank, w0, done in ((bk_gate, 0, gate_done), (bk_up, KT, up_done)):
                            split_product(pe, bank[h % 2][:, :],
                                          [((w_hi[:, w0 + k, c], w_lo[:, w0 + k, c]), (x_hi[:, k, :], x_lo[:, k, :]))
                                           for k in range(KT)]).then_inc(done, 1)
                    pe.wait_ge(y_added, ONE + TT * NFS * g + TT * s)
                    for h in range(HT):
                        pe.wait_ge(h_lo_ready, ONE + hidden(g, s, h))
                        for t in range(TT):
                            c = slice(t * P, t * P + P)
                            w = 2 * KT + h
                            pe.matmul(bk_y[t][:, :], h_hi[:, h, c], w_hi[:, w, :], start=(h == 0), stop=False)
                            pe.matmul(bk_y[t][:, :], h_hi[:, h, c], w_lo[:, w, :], start=False, stop=False)
                            mm = pe.matmul(bk_y[t][:, :], h_lo[:, h, c], w_hi[:, w, :], start=False, stop=(h == HT - 1))
                            if h == HT - 1:
                                mm.then_inc(y_done, 1)


def norm_and_store(nc, yacc, out):
    with ExitStack() as ctx:
        sb = lambda n, s, d=F32: ctx.enter_context(nc.sbuf_tensor(n, s, d))
        sem = lambda n: ctx.enter_context(nc.semaphore(n))
        stats, mv = sb("stats3", [P, NTILE, 6]), sb("mv3", [P, NTILE, 2])
        rstd, spare = sb("rstd3", [P, NTILE]), sb("spare3", [P, 2, NTILE])
        stat_ready, mv_ready, step, normed = (sem(n) for n in ("stat3", "mv3s", "ln_step3", "normed3"))
        stored = sem("out_stored")
        block = ctx.enter_context(nc.Block())

        @block.vector
        def _(dve):
            layernorm(dve, yacc, stats, mv, rstd, spare, stat_ready, mv_ready, step, normed)

        @block.sync
        def _(sp):
            with sp.Fori(0, NTILE // 2) as n:
                sp.wait_ge(normed, 2 * n + 2)
                sp.dma_start(out[:, bass.ds(2 * n, 2), :], yacc[:, bass.ds(2 * n, 2), :]).then_inc(stored, 16)
            sp.wait_ge(stored, 16 * NTILE // 2)


def program(nc, consts, x_tok, xt, wt, wo, gw, w13, w2t, w2f, x1t, out):
    with ExitStack() as ctx:
        yacc = ctx.enter_context(nc.sbuf_tensor("yacc", [P, NTILE, D], F32))
        out_tok = out.rearrange("b (n p) d -> p (b n) d", p=P)
        hadamard_of_w2(nc, consts, w2t, w2f)
        attention(nc, consts, x_tok.rearrange("b (n p) d -> p (b n) d", p=P), xt, wt, wo, gw, yacc)
        norm_and_turn(nc, consts, yacc, x1t)
        feed_forward(nc, x1t, w13, w2f, yacc)
        norm_and_store(nc, yacc, out_tok)


def kernel(**inputs):
    import concourse.bacc as _bacc
    from concourse.bass_utils import run_bass_kernel_spmd as _run

    f32 = np.float32
    x = np.asarray(inputs["L0_attn_hidden_states"])
    wq, wk, wv, wg, ws = (np.asarray(inputs["L0_attn_W" + c]) for c in "qkvgs")
    w1, w2, w3 = (np.asarray(inputs["L0_ffn_W" + c]) for c in "123")

    def tiles(w, n):
        return np.ascontiguousarray(w.reshape(KT, P, n, 512).transpose(0, 2, 1, 3))

    xt = np.ascontiguousarray(x.reshape(B, NB, ST, 2, 2, P).transpose(0, 1, 3, 5, 4, 2)).reshape(B, NB, 2, P, 512)
    groups = []
    for g in range(NG):
        side = np.concatenate([wq[:, g * HG * DK:(g + 1) * HG * DK], wk[:, g * HG * DK:(g + 1) * HG * DK],
                               ws[:, g * HG * M:(g + 1) * HG * M], wv[:, g * HG * DV:(g + 1) * HG * DV],
                               wg[:, g * HG * DV:(g + 1) * HG * DV]], axis=1)
        flat = side.reshape(KT, P, WC).transpose(1, 0, 2).reshape(P, WTILES, 512)
        groups.append(flat.transpose(1, 0, 2))
    wt = np.ascontiguousarray(np.stack(groups))
    wo = np.ascontiguousarray(np.asarray(inputs["L0_attn_Wo"]).reshape(NG, HG, P, D))
    gw = np.ascontiguousarray(np.asarray(inputs["L0_attn_g_norm_weight"]).reshape(P, 1))
    w13 = np.ascontiguousarray(np.stack([w.T.reshape(KT, P, NHG, 512).transpose(2, 0, 1, 3) for w in (w1, w3)],
                                        axis=1)).reshape(NHG, 2 * KT, P, 512)
    w2t = np.ascontiguousarray(w2.T.reshape(FF // P, P, 4, P).transpose(2, 1, 0, 3))
    had = np.array([[1.0]], f32)
    while had.shape[0] < P:
        had = np.block([[had, had], [had, -had]])
    consts = np.concatenate([np.eye(P, dtype=f32), np.triu(np.ones((P, P), f32)), had], axis=1).astype(f32)

    nc = _bacc.Bacc("TRN2", target_bir_lowering=False, num_devices=1)
    arrays = {"consts": consts, "x_tok": np.ascontiguousarray(x), "xt": xt, "wt": wt, "wo": wo, "gw": gw,
              "w13": w13, "w2t": w2t}
    aps = [nc.dram_tensor(n, a.shape, mybir.dt.from_np(a.dtype), kind="ExternalInput").ap() for n, a in arrays.items()]
    w2f = nc.dram_tensor("w2f", (FF // P, P, D), F32, kind="Internal").ap()
    x1t = nc.dram_tensor("x1t", (NFS, KT, P, TT * P), F32, kind="Internal").ap()
    out = nc.dram_tensor("out", (B, T, D), F32, kind="ExternalOutput").ap()
    program(nc, *aps, w2f, x1t, out)
    r = _run(nc, [arrays], core_ids=[0])
    return r.results[0]["out"]
```

```python
from contextlib import ExitStack

import numpy as np

import concourse.bass as bass
from concourse import mybir

ALU = mybir.AluOpType
ACT = mybir.ActivationFunctionType
AX_X = mybir.AxisListType.X
F32 = mybir.dt.float32
F32R = mybir.dt.float32r

P = 128
B, T, D = 2, 2048, 512
H, DK, DV, M = 16, 64, 128, 64
FF = 2048
EPS = 1e-5
CLAMP = 32.0
KT = D // P

HG = 4
NG = H // HG
PAIRS = HG // 2
ST = 2 * P
NB = T // ST
NCH = B * T // P
NST = B * T // ST
QC, KC, SC = 0, HG * DK, 2 * HG * DK
QKS = SC + HG * M
QKS_W = range(0, KT * QKS // 512)
V_W = range(QKS_W.stop, QKS_W.stop + KT)
G_W = range(V_W.stop, V_W.stop + KT)
O_W = range(G_W.stop, G_W.stop + HG)
PROJ_TILES, W_TILES = G_W.stop, O_W.stop
W_RING = 3

HT = 4
NHG = FF // (HT * P)
TT = 4
NFS = B * T // (TT * P)
NTILE = B * T // P
RING = 4
ONE = 1


def split_product(pe, out, terms):
    last = None
    for n, ((a_hi, a_lo), (b_hi, b_lo)) in enumerate(terms):
        pe.matmul(out, a_hi, b_hi, start=(n == 0), stop=False)
        pe.matmul(out, a_hi, b_lo, start=False, stop=False)
        last = pe.matmul(out, a_lo, b_hi, start=False, stop=(n == len(terms) - 1))
    return last


NEWTON = 1 + 3 * 3


def rsqrt(dve, x, y, a, step, base):
    dve.tensor_scalar(y.bitcast(mybir.dt.int32), x.bitcast(mybir.dt.int32), -0.5, float(0x5F375A86),
                      ALU.mult, ALU.add).then_inc(step, 1)
    for k in range(3):
        dve.wait_ge(step, base + (3 * k + 1))
        dve.tensor_tensor(a, y, y, ALU.mult).then_inc(step, 1)
        dve.wait_ge(step, base + (3 * k + 2))
        dve.scalar_tensor_tensor(out=a, in0=a, scalar=-0.5, in1=x, op0=ALU.mult, op1=ALU.mult).then_inc(step, 1)
        dve.wait_ge(step, base + (3 * k + 3))
        dve.scalar_tensor_tensor(out=y, in0=a, scalar=1.5, in1=y, op0=ALU.add, op1=ALU.mult).then_inc(step, 1)


def hadamard_of_w2(nc, consts, w2t, w2f):
    A = FF // P
    scale = float(np.float32(1.0 / np.sqrt(FF))) * 0.5
    NS = 4
    STEPS = (1, 2, 4, 8)
    with ExitStack() as ctx:
        sb = lambda n, s, d=F32: ctx.enter_context(nc.sbuf_tensor(n, s, d))
        sem = lambda n: ctx.enter_context(nc.semaphore(n))
        had = sb("had", [P, P])
        fly = [[sb(f"fly{s}_{j}", [P, A, P]) for j in range(2)] for s in range(2)]
        res = [sb(f"w2res{s}", [P, A, P]) for s in range(2)]
        bank = [ctx.enter_context(nc.psum_tensor(f"hbank{j}", [P, 4, P], F32)) for j in range(4)]
        had_in = sem("had_in")
        slice_in = [sem(f"slice_in{j}") for j in range(2)]
        fly_done = sem("fly_done")
        had_done = sem("had_done")
        scaled = sem("scaled")
        stored = [sem(f"w2_stored{j}") for j in range(2)]
        block = ctx.enter_context(nc.Block())

        @block.sync
        def _(sp):
            sp.dma_start(had[:, :], consts[:, 2 * P:3 * P]).then_inc(had_in, 16)
            for s in range(NS):
                if s >= 2:
                    sp.wait_ge(had_done, 4 * (s - 1))
                sp.dma_start(fly[s % 2][0][:, :, :], w2t[s]).then_inc(slice_in[s % 2], 16)
            for s in range(NS):
                sp.wait_ge(scaled, 4 * (s + 1))
                sp.dma_start(w2f[:, :, s * P:(s + 1) * P].rearrange("a p d -> p a d"),
                             res[s % 2][:, :, :]).then_inc(stored[s % 2], 16)
            for j in range(2):
                sp.wait_ge(stored[j], 16 * NS // 2)

        @block.vector
        def _(dve):
            n = 0
            for s in range(NS):
                dve.wait_ge(slice_in[s % 2], 16 * (s // 2 + 1))
                for j, h in enumerate(STEPS):
                    if j:
                        dve.wait_ge(fly_done, n)
                    src = fly[s % 2][j % 2][:, :, :].rearrange("p (n t h) d -> p n t h d", t=2, h=h)
                    dst = fly[s % 2][1 - j % 2][:, :, :].rearrange("p (n t h) d -> p n t h d", t=2, h=h)
                    for k in range(A // (2 * h)):
                        a, b = src[:, k, 0], src[:, k, 1]
                        dve.tensor_tensor(dst[:, k, 0], a, b, ALU.add).then_inc(fly_done, 1)
                        dve.tensor_tensor(dst[:, k, 1], a, b, ALU.subtract).then_inc(fly_done, 1)
                        n += 2

        @block.tensor
        def _(pe):
            pe.wait_ge(had_in, 16)
            per = sum(A // h for h in STEPS)
            for s in range(NS):
                pe.wait_ge(fly_done, per * (s + 1))
                for j in range(4):
                    if s:
                        pe.wait_ge(scaled, 4 * (s - 1) + j + 1)
                    pe.matmul(bank[j][:, :, :], had[:, :], fly[s % 2][0][:, 4 * j:4 * j + 4, :],
                              start=True, stop=True).then_inc(had_done, 1)

        @block.scalar
        def _(act):
            for s in range(NS):
                if s >= 2:
                    act.wait_ge(stored[s % 2], 16 * (s // 2))
                for j in range(4):
                    act.wait_ge(had_done, 4 * s + j + 1)
                    act.activation(res[s % 2][:, 4 * j:4 * j + 4, :], bank[j][:, :, :], ACT.Copy,
                                   scale=scale).then_inc(scaled, 1)


def attention(nc, consts, x_tok, xt, wt, wo, gw, yacc, ln):
    with ExitStack() as ctx:
        sb = lambda n, s, d=F32: ctx.enter_context(nc.sbuf_tensor(n, s, d))
        ps = lambda n, s: ctx.enter_context(nc.psum_tensor(n, s, F32))
        sem = lambda n: ctx.enter_context(nc.semaphore(n))

        cst = sb("cst", [P, 2, P])
        ident, causal = cst[:, 0, :], cst[:, 1, :]
        gwc = sb("gwc", [P, 1])
        qks_hi, qks_lo = sb("qks_hi", [P, KT, QKS], F32R), sb("qks_lo", [P, KT, QKS], F32R)
        wv_hi, wv_lo = sb("wv_hi", [P, KT, HG * DV], F32R), sb("wv_lo", [P, KT, HG * DV], F32R)
        wg_hi, wg_lo = sb("wg_hi", [P, KT, HG * DV], F32R), sb("wg_lo", [P, KT, HG * DV], F32R)
        wo_hi, wo_lo = sb("wo_hi", [P, HG, D], F32R), sb("wo_lo", [P, HG, D], F32R)
        w_stage = [sb(f"w_stage{j}", [P, 512]) for j in range(W_RING)]
        x_stage = [sb(f"x_stage{j}", [P, 512]) for j in range(2)]
        x_hi = [sb(f"x_hi{b}", [P, KT, ST], F32R) for b in range(B)]
        x_lo = [sb(f"x_lo{b}", [P, KT, ST], F32R) for b in range(B)]
        qT = [sb(f"qT{b}", [P, PAIRS, ST]) for b in range(B)]
        kT = [sb(f"kT{b}", [P, PAIRS, ST]) for b in range(B)]
        eT = [sb(f"eT{b}", [P, PAIRS, ST]) for b in range(B)]
        zT = [sb(f"zT{b}", [P, PAIRS, ST]) for b in range(B)]
        carry = [sb(f"carry{b}", [P, PAIRS]) for b in range(B)]
        ke = sb("ke", [P, 2, PAIRS, P])
        k_tok, e_tok = ke[:, 0], ke[:, 1]
        rz = sb("rz", [P, HG, M])
        v_tok = sb("v_tok", [P, HG, DV])
        gate = sb("gate", [P, HG * DV])
        qk = sb("qk", [P, 2, PAIRS, P])
        ep = sb("ep", [P, 2, PAIRS, P])
        sm = sb("sm", [P, HG, M])
        pv = sb("pv", [P, HG, M])
        pvT = sb("pvT", [P, PAIRS, P])
        hk = [sb(f"hk{b}", [P, PAIRS, 2 * M]) for b in range(B)]
        hv = [sb(f"hv{b}", [P, PAIRS, 2 * DV]) for b in range(B)]
        ow = sb("ow", [P, HG, DV])
        oT_hi, oT_lo = sb("oT_hi", [P, HG * P], F32R), sb("oT_lo", [P, HG * P], F32R)
        row_max, row_sum, row_rcp = sb("row_max", [P, HG]), sb("row_sum", [P, HG]), sb("row_rcp", [P, HG])
        ssq, t1, t2, t3, fac = (sb(n, [P, HG]) for n in ("ssq", "t1", "t2", "t3", "fac"))

        bk_v = ps("bk_v", [P, 512])
        bk_g = ps("bk_g", [P, 512])
        bk_ab = [ps(f"bk_ab{e}", [P, 2, PAIRS, P]) for e in range(2)]
        bk_ok = ps("bk_ok", [P, 512])
        bk_ov = ps("bk_ov", [P, HG, DV])
        bk_t = ps("bk_t", [P, 512])
        bk_u = ps("bk_u", [P, 512])

        cst_in, x_in = sem("cst_in"), sem("x_in")
        w_staged = [sem(f"w_staged{j}") for j in range(W_RING)]
        x_staged = [sem(f"x_staged{j}") for j in range(2)]
        w_hi_ready, w_lo_ready = sem("w_hi_ready"), sem("aw_lo_ready")
        x_hi_ready, x_lo_ready = sem("x_hi_ready"), sem("ax_lo_ready")
        s_done, q_done, k_done = sem("s_done"), sem("q_done"), sem("k_done")
        clipped, e_ready, scanned, z_ready = sem("clipped"), sem("e_ready"), sem("scanned"), sem("z_ready")
        carried = sem("carried")
        q_ready, k_ready = sem("q_ready"), sem("k_ready")
        ke_done, ke_ready = sem("ke_done"), sem("ke_ready")
        qk_done, qk_ready = sem("qk_done"), sem("qk_ready")
        rz_done, rz_ready = sem("rz_done"), sem("rz_ready")
        v_done, v_ready = sem("v_done"), sem("v_ready")
        ok_done, okz_ready, max_ready, sub_ready = sem("ok_done"), sem("okz_ready"), sem("max_ready"), sem("sub_ready")
        exp_ready, sum_ready, pv_ready = sem("exp_ready"), sem("sum_ready"), sem("pv_ready")
        rcp_ready = sem("rcp_ready")
        hk_done, hk_ready = sem("hk_done"), sem("hk_ready")
        g_done, tanh_ready, gate_ready = sem("g_done"), sem("tanh_ready"), sem("gate_ready")
        pvT_done, pvT_ready = sem("pvT_done"), sem("pvT_ready")
        ep_done, ep_ready = sem("ep_done"), sem("ep_ready")
        ov_done, sq_ready, ssq_ready = sem("ov_done"), sem("sq_ready"), sem("ssq_ready")
        t1_ready, t2_ready, t3_ready, fac_ready = sem("t1_ready"), sem("t2_ready"), sem("t3_ready"), sem("fac_ready")
        ow_ready = sem("ow_ready")
        hv_done, hv_ready = sem("hv_done"), sem("hv_ready")
        oT_done, oT_hi_ready, oT_lo_ready = sem("oT_done"), sem("oT_hi_ready"), sem("oT_lo_ready")
        y_done, y_added = sem("y_done"), sem("y_added")
        zeroed, newton = sem("zeroed"), sem("newton")
        ln_stat, ln_mv, ln_var, ln_newton = sem("ln_stat"), sem("ln_mv"), sem("ln_var"), sem("ln_newton")

        def every_step(eng, one_step):
            one_step(0, 0)
            with eng.Fori(0, NG - 1) as g:
                with eng.Fori(1, NB - 1) as i:
                    one_step(g, i)
                one_step(g, NB - 1)
                one_step(g + 1, 0)
            with eng.Fori(1, NB - 1) as i:
                one_step(NG - 1, i)
            one_step(NG - 1, NB - 1)

        def is_at(value, at):
            return isinstance(value, int) and value == at

        def parts(w):
            if w in QKS_W:
                c = slice(512 * w, 512 * w + 512)
                return [t[:, :, :].rearrange("p k c -> p (k c)")[:, c] for t in (qks_hi, qks_lo)]
            hi, lo, first = ((wv_hi, wv_lo, V_W.start) if w in V_W else
                             (wg_hi, wg_lo, G_W.start) if w in G_W else (wo_hi, wo_lo, O_W.start))
            return [hi[:, w - first, :], lo[:, w - first, :]]

        def chunk(g, i, r):
            return NCH * g + 4 * i + (r + 1)

        def super_(g, i, b):
            return NST * g + 2 * i + (b + 1)

        def x_tile(g, i, b, half):
            return 2 * NST * g + 4 * i + (2 * b + half + 1)

        def w_tile(g, w):
            return W_TILES * g + (w + 1)

        block = ctx.enter_context(nc.Block())

        @block.sync
        def _(sp):
            sp.dma_start(cst[:, :, :], consts[:, 0:2 * P].rearrange("p (a c) -> p a c", a=2)).then_inc(cst_in, 16)
            sp.dma_start(gwc[:, :], gw).then_inc(cst_in, 16)

            def load_w(g, w):
                sp.wait_ge(w_lo_ready, ONE + W_TILES * g + max(w + 1 - W_RING, 0))
                src = wt[g, w] if w < PROJ_TILES else wo[g, w - PROJ_TILES]
                sp.dma_start(w_stage[w % W_RING][:, :], src).then_inc(w_staged[w % W_RING], 16)

            def load_x(g, i, b):
                sp.wait_ge(x_lo_ready, ONE + x_tile(g, i, b, 0) - 1)
                for half in range(2):
                    sp.dma_start(x_stage[half][:, :], xt[b, i, half]).then_inc(x_staged[half], 16)

            with sp.Fori(0, NG) as g:
                for w in QKS_W[:3]:
                    load_w(g, w)
                load_x(g, 0, 0)
                for w in [*QKS_W[3:], *V_W, *G_W]:
                    load_w(g, w)
                load_x(g, 0, 1)
                for w in O_W[:3]:
                    load_w(g, w)
                load_x(g, 1, 0)
                for w in O_W[3:]:
                    load_w(g, w)
                load_x(g, 1, 1)
                with sp.Fori(2, NB) as i:
                    for b in range(B):
                        load_x(g, i, b)

        @block.gpsimd
        def _(pool):
            for c in range(4):
                pool.dma_start(yacc[:, 8 * c:8 * c + 8, :], x_tok[:, 8 * c:8 * c + 8, :]).then_inc(x_in, 16)

            with pool.Fori(0, NG * NB) as i:
                for b in range(B):
                    for half in range(2):
                        pool.wait_ge(x_hi_ready, x_tile(0, i, b, half))
                        dst = slice(half * 2, half * 2 + 2)
                        pool.tensor_tensor(x_lo[b][:, dst, :].rearrange("p k t -> p (k t)"), x_stage[half][:, :],
                                           x_hi[b][:, dst, :].rearrange("p k t -> p (k t)"), ALU.subtract)\
                            .then_inc(x_lo_ready, 1)

        @block.scalar
        def _(act):
            act.wait_ge(cst_in, 32)

            def x_high(g, i, b):
                for half in range(2):
                    act.wait_ge(x_staged[half], super_(g, i, b) * 16)
                    act.activation(x_hi[b][:, half * 2:half * 2 + 2, :].rearrange("p k t -> p (k t)"),
                                   x_stage[half][:, :], ACT.Copy).then_inc(x_hi_ready, 1)

            def w_high(g, *tiles):
                for w in tiles:
                    act.wait_ge(w_staged[w % W_RING], (W_TILES // W_RING * g + (w // W_RING + 1)) * 16)
                    if w in O_W:
                        act.activation(parts(w)[0], w_stage[w % W_RING][:, :], ACT.Copy, scale=gwc[:, 0:1])\
                            .then_inc(w_hi_ready, 1)
                    else:
                        act.activation(parts(w)[0], w_stage[w % W_RING][:, :], ACT.Copy).then_inc(w_hi_ready, 1)

            def exp_s(g, i, b):
                act.wait_ge(clipped, super_(g, i, b))
                act.activation(eT[b][:, :, :], eT[b][:, :, :], ACT.Exp).then_inc(e_ready, 1)

            def q_copy(g, i, b):
                act.wait_ge(q_done, super_(g, i, b))
                act.activation(qT[b][:, :, :], bk_g[:, :].rearrange("p (a t) -> p a t", a=PAIRS), ACT.Copy)\
                    .then_inc(q_ready, 1)

            def k_copy(g, i, b):
                act.wait_ge(k_done, super_(g, i, b))
                act.activation(kT[b][:, :, :], bk_v[:, :].rearrange("p (a t) -> p a t", a=PAIRS), ACT.Copy)\
                    .then_inc(k_ready, 1)

            def square_o(g, i, r):
                act.wait_ge(ov_done, chunk(g, i, r))
                act.activation(ow[:, :, :], bk_ov[:, :, :], ACT.Square).then_inc(sq_ready, 1)

            def o_high(g, i, r):
                act.wait_ge(oT_done, chunk(g, i, r))
                act.activation(oT_hi[:, :], bk_t[:, :], ACT.Copy).then_inc(oT_hi_ready, 1)

            w_high(0, *QKS_W)
            x_high(0, 0, 0)
            w_high(0, *V_W)
            exp_s(0, 0, 0)
            w_high(0, *G_W[:2])
            q_copy(0, 0, 0)
            k_copy(0, 0, 0)

            def one_step(g, i):
                start, end, last = is_at(i, 0), is_at(i, NB - 1), is_at(g, NG - 1)
                for r in range(4):
                    b = r // 2
                    n = chunk(g, i, r)
                    nxt = (i, 1) if r < 2 else (i + 1, 0)
                    more = not (end and last and r >= 2)
                    reload = end and r >= 2 and not last
                    if not (start and is_at(g, 0) and r < 2):
                        o_high(g, i, r - 2)
                    if start and r == 2:
                        if not is_at(g, 0):
                            act.wait_ge(y_done, ONE + NCH * g)
                        w_high(g, *O_W[:2])
                    if not (start and is_at(g, 0) and r == 0):
                        square_o(g, i, r - 1)
                    if start and r == 2:
                        w_high(g, *O_W[2:])
                    if reload and r == 2:
                        w_high(g + 1, *QKS_W[:2])
                    if r % 2 == 0 and more:
                        act.wait_ge(g_done, ONE + n - 1)
                        x_high(g, *nxt)
                    if reload and r == 2:
                        w_high(g + 1, QKS_W[2])
                    if start and r == 0:
                        w_high(g, *G_W[2:])
                    act.wait_ge(ke_done, n)
                    act.activation(ke[:, :, :, :], bk_t[:, :].rearrange("p (a c t) -> p a c t", a=2, c=2),
                                   ACT.Copy).then_inc(ke_ready, 1)
                    if reload and r == 2:
                        w_high(g + 1, QKS_W[3])
                    act.wait_ge(rz_done, n)
                    act.activation(rz[:, :, :], bk_u[:, 0:HG * M].rearrange("p (h m) -> p h m", h=HG),
                                   ACT.Copy).then_inc(rz_ready, 1)
                    if reload and r == 2:
                        w_high(g + 1, QKS_W[4])
                    act.wait_ge(v_done, n)
                    act.activation(v_tok[:, :, :], bk_v[:, :].rearrange("p (h v) -> p h v", h=HG),
                                   ACT.Copy).then_inc(v_ready, 1)
                    if reload and r == 2:
                        w_high(g + 1, QKS_W[5])
                    act.wait_ge(sub_ready, n)
                    act.activation(sm[:, :, :], sm[:, :, :], ACT.Exp, scale=DK ** -0.5).then_inc(exp_ready, 1)
                    if reload and r == 3:
                        w_high(g + 1, *V_W[:2])
                    act.wait_ge(g_done, ONE + n)
                    act.wait_ge(ow_ready, ONE + HG * (n - 1))
                    act.activation(gate[:, :], bk_g[:, :], ACT.Tanh, scale=0.5).then_inc(tanh_ready, 1)
                    if reload and r == 3:
                        w_high(g + 1, *V_W[2:])
                    act.wait_ge(pvT_done, n)
                    act.activation(pvT[:, :, :], bk_ok[:, 256:512].rearrange("p (a t) -> p a t", a=PAIRS),
                                   ACT.Copy).then_inc(pvT_ready, 1)
                    if reload and r == 3:
                        w_high(g + 1, *G_W[:2])
                    if more:
                        if r % 2 == 0:
                            exp_s(g, *nxt)
                        else:
                            q_copy(g, *nxt)
                            k_copy(g, *nxt)

            every_step(act, one_step)
            o_high(NG - 1, NB - 1, 2)
            square_o(NG - 1, NB - 1, 3)
            o_high(NG - 1, NB - 1, 3)

        @block.vector
        def _(dve):
            dve.wait_ge(cst_in, 32)
            dve.wait_ge(x_in, 64)

            def clip_s(g, i, b):
                dve.wait_ge(s_done, super_(g, i, b))
                dve.tensor_scalar(eT[b][:, :, :], bk_g[:, :].rearrange("p (a t) -> p a t", a=PAIRS),
                                  CLAMP, -CLAMP, ALU.min, ALU.max).then_inc(clipped, 1)

            def scan_e(g, i, b):
                dve.wait_ge(e_ready, super_(g, i, b))
                for a in range(PAIRS):
                    dve.tensor_tensor_scan(zT[b][:, a, :], eT[b][:, a, :], eT[b][:, a, :], carry[b][:, a:a + 1],
                                           ALU.add, ALU.max).then_inc(scanned, 1)
                dve.wait_ge(scanned, 2 * super_(g, i, b))
                dve.tensor_copy(carry[b][:, :], zT[b][:, :, ST - 1]).then_inc(carried, 1)

            def invert_z(g, i, b):
                dve.wait_ge(carried, super_(g, i, b))
                dve.reciprocal(zT[b][:, :, :], zT[b][:, :, :]).then_inc(z_ready, 1)

            def update_hv(g, i, r):
                b = r % 4 // 2
                dve.wait_ge(hv_done, chunk(g, i, r))
                upd = bk_u[:, :].rearrange("p (a c) -> p a c", a=PAIRS)
                for e in range(2):
                    rows, cols = slice(64 * e, 64 * e + 64), slice(DV * e, DV * e + DV)
                    dve.tensor_tensor(hv[b][rows, :, cols], hv[b][rows, :, cols], upd[rows, :, cols], ALU.add)\
                        .then_inc(hv_ready, 1)

            def update_hk(g, i, r):
                b = r // 2
                dve.wait_ge(hk_done, chunk(g, i, r))
                upd = bk_u[:, 256:512].rearrange("p (a c) -> p a c", a=PAIRS)
                for e in range(2):
                    rows, cols = slice(64 * e, 64 * e + 64), slice(M * e, M * e + M)
                    dve.tensor_tensor(hk[b][rows, :, cols], hk[b][rows, :, cols], upd[rows, :, cols], ALU.add)\
                        .then_inc(hk_ready, 1)

            def factor_o(g, i, r):
                n = chunk(g, i, r)
                dve.wait_ge(sq_ready, n)
                dve.tensor_reduce(ssq[:, :], ow[:, :, :], AX_X, ALU.add).then_inc(ssq_ready, 1)
                dve.wait_ge(ssq_ready, n)
                dve.wait_ge(rcp_ready, n)
                dve.tensor_tensor(t1[:, :], ssq[:, :], row_rcp[:, :], ALU.mult).then_inc(t1_ready, 1)
                dve.wait_ge(t1_ready, n)
                dve.tensor_tensor(t2[:, :], t1[:, :], row_rcp[:, :], ALU.mult).then_inc(t2_ready, 1)
                dve.wait_ge(t2_ready, n)
                dve.tensor_scalar(t1[:, :], t2[:, :], 1.0, DV * EPS, ALU.mult, ALU.add).then_inc(t3_ready, 1)
                dve.wait_ge(t3_ready, n)
                rsqrt(dve, t1[:, :], t3[:, :], t2[:, :], newton, NEWTON * (n - 1))
                dve.wait_ge(newton, NEWTON * n)
                dve.scalar_tensor_tensor(out=fac[:, :], in0=t3[:, :], scalar=0.5 * DV ** 0.5, in1=row_rcp[:, :],
                                         op0=ALU.mult, op1=ALU.mult).then_inc(fac_ready, 1)

            def gate_o(g, i, r):
                n = chunk(g, i, r)
                dve.wait_ge(fac_ready, n)
                dve.wait_ge(gate_ready, ONE + n)
                for h in range(HG):
                    dve.scalar_tensor_tensor(out=ow[:, h, :], in0=bk_ov[:, h, :], scalar=fac[:, h:h + 1],
                                             in1=gate[:, h * DV:(h + 1) * DV], op0=ALU.mult, op1=ALU.mult)\
                        .then_inc(ow_ready, 1)

            def o_low(g, i, r):
                dve.wait_ge(oT_hi_ready, chunk(g, i, r))
                dve.tensor_tensor(oT_lo[:, :], bk_t[:, :], oT_hi[:, :], ALU.subtract).then_inc(oT_lo_ready, 1)

            def add_y(g, i, r):
                before = (NB if is_at(i, 0) else i) - 1 if r < 0 else i
                at = T // P * (r % 4 // 2) + 2 * before + r % 2
                dve.wait_ge(y_done, ONE + chunk(g, i, r))
                dve.tensor_tensor(yacc[:, at, :], yacc[:, at, :], bk_v[:, :], ALU.add).then_inc(y_added, 1)

            stats, mv, var, rstd, spare = ln
            after = spare[:, 0:1]

            def norm_rows(s, r, part):
                tiles = [T // P * part + 2 * s + half for half in range(2)]
                if r == 1:
                    dve.wait_ge(y_added, ONE + chunk(NG - 1, s, 1 + 2 * part))
                    if not isinstance(s, int):
                        dve.memset(after, 0.0)
                    for j, t in enumerate(tiles, 2 * part):
                        dve.bn_stats(stats[:, j, :], yacc[:, t, :]).then_inc(ln_stat, 1)
                if r == 2 and part == 0:
                    dve.wait_ge(ln_stat, 4 * s + 4)
                    if not isinstance(s, int):
                        dve.memset(after, 0.0)
                    for j in range(4):
                        dve.bn_aggr(mv[:, j, :], stats[:, j, :]).then_inc(ln_mv, 1)
                    dve.wait_ge(ln_mv, 4 * s + 4)
                    dve.tensor_scalar(var[:, :], mv[:, :, 1], 1.0, EPS, ALU.mult, ALU.add).then_inc(ln_var, 1)
                if r == 2 and part == 1:
                    dve.wait_ge(ln_var, s + 1)
                    rsqrt(dve, var[:, :], rstd[:, :], spare[:, :], ln_newton, NEWTON * s)
                if r == 3:
                    dve.wait_ge(ln_newton, NEWTON * s + NEWTON)
                    for j, t in enumerate(tiles, 2 * part):
                        dve.tensor_scalar(yacc[:, t, :], yacc[:, t, :], mv[:, j, 0:1], rstd[:, j:j + 1],
                                          ALU.subtract, ALU.mult)

            def w_low(g, *tiles):
                for w in tiles:
                    hi, lo = parts(w)
                    dve.wait_ge(w_hi_ready, w_tile(g, w))
                    if w in O_W:
                        dve.scalar_tensor_tensor(out=lo, in0=w_stage[w % W_RING][:, :], scalar=gwc[:, 0:1], in1=hi,
                                                 op0=ALU.mult, op1=ALU.subtract).then_inc(w_lo_ready, 1)
                    else:
                        dve.tensor_tensor(lo, w_stage[w % W_RING][:, :], hi, ALU.subtract).then_inc(w_lo_ready, 1)

            def zero_states(b):
                for t in (hk[b][:, :, :], hv[b][:, :, :], carry[b][:, :]):
                    dve.memset(t, 0.0).then_inc(zeroed, 1)

            w_low(0, *QKS_W)
            zero_states(0)
            zero_states(1)
            clip_s(0, 0, 0)
            w_low(0, *V_W)
            dve.wait_ge(zeroed, 6)
            scan_e(0, 0, 0)
            invert_z(0, 0, 0)
            w_low(0, *G_W[:2])

            def one_step(g, i):
                start, end, last = is_at(i, 0), is_at(i, NB - 1), is_at(g, NG - 1)
                for r in range(4):
                    b = r // 2
                    n = chunk(g, i, r)
                    nxt = (i, 1) if r < 2 else (i + 1, 0)
                    first = start and is_at(g, 0) and r == 0
                    behind = start and is_at(g, 0) and r < 2
                    more = not (end and last and r >= 2)
                    reload = end and r >= 2 and not last
                    if not behind:
                        o_low(g, i, r - 2)
                    if start and r == 2:
                        w_low(g, O_W[0])
                    if not first:
                        update_hv(g, i, r - 1)
                    if start and r == 2:
                        w_low(g, O_W[1])
                    if reload and r == 2:
                        w_low(g + 1, QKS_W[0])
                    dve.wait_ge(qk_done, n)
                    mask = causal.unsqueeze(1).broadcast_to([P, PAIRS, P])
                    for e in range(2):
                        dve.tensor_tensor(qk[:, e], bk_ab[e][:, 0], mask, ALU.mult).then_inc(qk_ready, 1)
                    if start and r == 2:
                        w_low(g, *O_W[2:])
                    if start and r == 0:
                        w_low(g, *G_W[2:])
                    if reload and r == 2:
                        w_low(g + 1, QKS_W[1])
                    if (reload and r == 2) or (start and r == 0 and not first):
                        dve.wait_ge(hv_ready, ONE + 2 * n - 2)
                        dve.wait_ge(hk_ready, ONE + 2 * n - 2)
                        zero_states(0 if reload else 1)
                    if not first:
                        factor_o(g, i, r - 1)
                    if reload and r == 2:
                        w_low(g + 1, QKS_W[2])
                    if r % 2 == 1 and more:
                        if (start and r == 1) or (end and r == 3):
                            dve.wait_ge(zeroed, 6 * g + (6 if r == 1 else 9))
                        scan_e(g, *nxt)
                    dve.wait_ge(ok_done, n)
                    dve.wait_ge(rz_ready, n)
                    dve.tensor_tensor(sm[:, :, :], bk_ok[:, 0:HG * M].rearrange("p (h m) -> p h m", h=HG),
                                      rz[:, :, :], ALU.mult).then_inc(okz_ready, 1)
                    dve.wait_ge(okz_ready, n)
                    dve.tensor_reduce(row_max[:, :], sm[:, :, :], AX_X, ALU.max).then_inc(max_ready, 1)
                    dve.wait_ge(max_ready, n)
                    dve.tensor_tensor(sm[:, :, :], sm[:, :, :], row_max[:, :].unsqueeze(2).broadcast_to([P, HG, M]),
                                      ALU.subtract).then_inc(sub_ready, 1)
                    if reload and r == 2:
                        w_low(g + 1, QKS_W[3])
                    if not first:
                        gate_o(g, i, r - 1)
                    update_hk(g, i, r)
                    if reload and r == 2:
                        w_low(g + 1, QKS_W[4])
                    if reload and r == 3:
                        w_low(g + 1, V_W[0])
                    dve.wait_ge(exp_ready, n)
                    dve.tensor_tensor(pv[:, :, :], sm[:, :, :], rz[:, :, :], ALU.mult).then_inc(pv_ready, 1)
                    dve.tensor_reduce(row_sum[:, :], sm[:, :, :], AX_X, ALU.add).then_inc(sum_ready, 1)
                    if reload and r == 2:
                        w_low(g + 1, QKS_W[5])
                    if reload and r == 3:
                        w_low(g + 1, V_W[1])
                    dve.wait_ge(sum_ready, n)
                    dve.reciprocal(row_rcp[:, :], row_sum[:, :]).then_inc(rcp_ready, 1)
                    dve.wait_ge(tanh_ready, n)
                    dve.scalar_tensor_tensor(out=gate[:, :], in0=gate[:, :], scalar=1.0, in1=bk_g[:, :],
                                             op0=ALU.add, op1=ALU.mult).then_inc(gate_ready, 1)
                    if last and r:
                        norm_rows(i - 1, r, 0)
                    if not behind:
                        add_y(g, i, r - 2)
                    if reload and r == 3:
                        w_low(g + 1, *V_W[2:])
                    if r % 2 == 1 and more:
                        invert_z(g, *nxt)
                    dve.wait_ge(ep_done, n)
                    for e in range(2):
                        dve.tensor_tensor(ep[:, e], bk_ab[e][:, 1], mask, ALU.mult).then_inc(ep_ready, 1)
                    if reload and r == 3:
                        w_low(g + 1, *G_W[:2])
                    if r % 2 == 0 and more:
                        clip_s(g, *nxt)
                    if last and r:
                        norm_rows(i - 1, r, 1)

            every_step(dve, one_step)
            o_low(NG - 1, NB - 1, 2)
            update_hv(NG - 1, NB - 1, 3)
            factor_o(NG - 1, NB - 1, 3)
            gate_o(NG - 1, NB - 1, 3)
            add_y(NG - 1, NB - 1, 2)
            o_low(NG - 1, NB - 1, 3)
            add_y(NG - 1, NB - 1, 3)

        @block.tensor
        def _(pe):
            for started in (w_lo_ready, x_lo_ready, g_done, y_done, gate_ready, y_added, oT_lo_ready, ep_ready, hv_ready, hk_ready,
                            pvT_ready, ow_ready):
                pe.sem_inc(started, ONE)
            pe.wait_ge(cst_in, 32)

            def transposed(out, b, col, a):
                c = slice(col + a * P, col + a * P + P)
                return split_product(pe, out[:, a * ST:(a + 1) * ST],
                                     [((qks_hi[:, k, c], qks_lo[:, k, c]), (x_hi[b][:, k, :], x_lo[b][:, k, :]))
                                      for k in range(KT)])

            def by_token(out, b, half, hi, lo):
                t = slice(half * P, half * P + P)
                return split_product(pe, out[:, :],
                                     [((x_hi[b][:, k, t], x_lo[b][:, k, t]), (hi[:, k, :], lo[:, k, :]))
                                      for k in range(KT)])

            def values(g, i, r):
                b = r % 4 // 2
                n = chunk(g, i, r)
                pe.wait_ge(ep_ready, ONE + 2 * n)
                pe.wait_ge(hv_ready, ONE + 2 * n - 2)
                pe.wait_ge(ow_ready, ONE + 4 * n - 4)
                pe.wait_ge(v_ready, n)
                for a in range(PAIRS):
                    pe.matmul(bk_ov[:, 2 * a:2 * a + 2, :], pvT[:, a, :], hv[b][:, a, :].rearrange("p (e v) -> p e v", e=2),
                              start=True, stop=False)
                    for e in range(2):
                        mm = pe.matmul(bk_ov[:, 2 * a + e, :], ep[:, e, a, :], v_tok[:, 2 * a + e, :],
                                       start=False, stop=(e == 1))
                mm.then_inc(ov_done, 1)
                pe.wait_ge(hk_ready, ONE + 2 * n)
                for a in range(PAIRS):
                    mm = pe.matmul(bk_u[:, 256 * a:256 * a + 256], e_tok[:, a, :],
                                   v_tok[:, 2 * a:2 * a + 2, :].rearrange("p h v -> p (h v)"), start=True, stop=True)
                mm.then_inc(hv_done, 1)

            def turn_o(g, i, r):
                n = chunk(g, i, r)
                pe.wait_ge(ow_ready, ONE + 4 * n)
                for h in range(HG):
                    mm = pe.transpose(bk_t[:, P * h:P * h + P], ow[:, h, :], ident)
                mm.then_inc(oT_done, 1)

            def project_y(g, i, r):
                pe.wait_ge(oT_lo_ready, ONE + chunk(g, i, r))
                split_product(pe, bk_v[:, :], [((oT_hi[:, P * h:P * h + P], oT_lo[:, P * h:P * h + P]),
                                                (wo_hi[:, h, :], wo_lo[:, h, :])) for h in range(HG)])\
                    .then_inc(y_done, 1)

            pe.wait_ge(w_lo_ready, ONE + w_tile(0, QKS_W[-1]))
            pe.wait_ge(x_lo_ready, ONE + x_tile(0, 0, 0, 1))
            for a in range(PAIRS):
                mm = transposed(bk_g, 0, SC, a)
            mm.then_inc(s_done, 1)
            for a in range(PAIRS):
                mm = transposed(bk_v, 0, KC, a)
            mm.then_inc(k_done, 1)
            pe.wait_ge(clipped, 1)
            for a in range(PAIRS):
                mm = transposed(bk_g, 0, QC, a)
            mm.then_inc(q_done, 1)

            def one_step(g, i):
                start, end, last = is_at(i, 0), is_at(i, NB - 1), is_at(g, NG - 1)
                for r in range(4):
                    b, half = r // 2, r % 2
                    n = chunk(g, i, r)
                    nxt = (i, 1) if r < 2 else (i + 1, 0)
                    nb = 1 - b
                    m = super_(g, *nxt)
                    first = start and is_at(g, 0) and r == 0
                    more = not (end and last and r >= 2)
                    t = slice(half * P, half * P + P)
                    behind = start and is_at(g, 0) and r < 2
                    if not behind:
                        pe.wait_ge(ke_ready, n - 1)
                        turn_o(g, i, r - 2)
                    if not first:
                        values(g, i, r - 1)
                    if half == 0:
                        pe.wait_ge(k_ready, super_(g, i, b))
                        pe.wait_ge(e_ready, super_(g, i, b))
                        pe.wait_ge(q_ready, super_(g, i, b))
                        pe.wait_ge(z_ready, super_(g, i, b))
                    if not behind:
                        pe.wait_ge(oT_lo_ready, ONE + n - 2)
                    elif r == 1:
                        pe.wait_ge(ke_ready, n - 1)
                    for a in range(PAIRS):
                        pe.transpose(bk_t[:, P * a:P * a + P], kT[b][:, a, t], ident)
                    for a in range(PAIRS):
                        mm = pe.transpose(bk_t[:, 256 + P * a:256 + P * a + P], eT[b][:, a, t], ident)
                    mm.then_inc(ke_done, 1)
                    pe.wait_ge(ep_ready, ONE + 2 * n - 2)
                    for a in range(PAIRS):
                        for e in range(2):
                            rows = slice(64 * e, 64 * e + 64)
                            mm = pe.matmul(bk_ab[e][:, 0, a, :], kT[b][rows, a, t], qT[b][rows, a, t],
                                           start=True, stop=True)
                    mm.then_inc(qk_done, 1)
                    pe.wait_ge(hv_ready, ONE + 2 * n - 2)
                    for a in range(PAIRS):
                        mm = pe.transpose(bk_u[:, P * a:P * a + P], zT[b][:, a, t], ident)
                    mm.then_inc(rz_done, 1)
                    if half == 0:
                        pe.wait_ge(k_ready, super_(g, i, b))
                    elif behind:
                        pe.wait_ge(v_ready, n - 1)
                    else:
                        pe.wait_ge(y_added, ONE + n - 3)
                    if start and r == 0:
                        pe.wait_ge(w_lo_ready, ONE + w_tile(g, V_W[-1]))
                    by_token(bk_v, b, half, wv_hi, wv_lo).then_inc(v_done, 1)
                    pe.wait_ge(qk_ready, 2 * n)
                    pe.wait_ge(ke_ready, n)
                    pe.wait_ge(hk_ready, ONE + 2 * n - 2)
                    pe.wait_ge(pvT_ready, ONE + n - 1)
                    if start and half == 0:
                        pe.wait_ge(zeroed, 6 * g + 3 * (b + 1))
                    for a in range(PAIRS):
                        pe.matmul(bk_ok[:, P * a:P * a + P], qT[b][:, a, t], hk[b][:, a, :], start=True, stop=False)
                        for e in range(2):
                            o = P * a + M * e
                            mm = pe.matmul(bk_ok[:, o:o + M], qk[:, e, a, :], e_tok[:, a, M * e:M * e + M],
                                           start=False, stop=(e == 1))
                    mm.then_inc(ok_done, 1)
                    pe.wait_ge(rz_ready, n)
                    for a in range(PAIRS):
                        mm = pe.matmul(bk_u[:, 256 + P * a:256 + P * a + P], k_tok[:, a, :], e_tok[:, a, :],
                                       start=True, stop=True)
                    mm.then_inc(hk_done, 1)
                    if half == 0:
                        pe.wait_ge(q_ready, super_(g, i, b))
                    elif more:
                        pe.wait_ge(clipped, m)
                    else:
                        pe.wait_ge(gate_ready, ONE + n - 1)
                    if start and r == 0:
                        pe.wait_ge(w_lo_ready, ONE + w_tile(g, G_W[-1]))
                    by_token(bk_g, b, half, wg_hi, wg_lo).then_inc(g_done, 1)
                    pe.wait_ge(v_ready, n)
                    if start and r == 2:
                        pe.wait_ge(w_lo_ready, ONE + w_tile(g, O_W[-1]))
                    if not behind:
                        project_y(g, i, r - 2)
                    pe.wait_ge(pv_ready, n)
                    for a in range(PAIRS):
                        mm = pe.transpose(bk_ok[:, 256 + P * a:256 + P * a + P],
                                          pv[:, 2 * a:2 * a + 2, :].rearrange("p h m -> p (h m)"), ident)
                    mm.then_inc(pvT_done, 1)
                    if more:
                        pe.wait_ge(gate_ready, ONE + n)
                        if half == 0:
                            pe.wait_ge(x_lo_ready, ONE + x_tile(g, *nxt, 1))
                            if end and r == 2:
                                pe.wait_ge(w_lo_ready, ONE + w_tile(g + 1, QKS_W[-1]))
                        transposed(bk_g, nb, SC if half == 0 else QC, 0)
                    pe.wait_ge(pvT_ready, ONE + n)
                    pe.wait_ge(qk_ready, 2 * n)
                    for a in range(PAIRS):
                        for e in range(2):
                            rows = slice(64 * e, 64 * e + 64)
                            mm = pe.matmul(bk_ab[e][:, 1, a, :], eT[b][rows, a, t], pvT[rows, a, :],
                                           start=True, stop=True)
                    mm.then_inc(ep_done, 1)
                    if more:
                        mm = transposed(bk_g, nb, SC if half == 0 else QC, 1)
                        mm.then_inc(s_done if half == 0 else q_done, 1)
                        if half == 1:
                            if not behind:
                                pe.wait_ge(y_added, ONE + n - 2)
                            for a in range(PAIRS):
                                mm = transposed(bk_v, nb, KC, a)
                            mm.then_inc(k_done, 1)

            every_step(pe, one_step)
            pe.wait_ge(ke_ready, chunk(NG - 1, NB - 1, 3))
            turn_o(NG - 1, NB - 1, 2)
            values(NG - 1, NB - 1, 3)
            pe.wait_ge(y_added, ONE + chunk(NG - 1, NB - 1, 1))
            project_y(NG - 1, NB - 1, 2)
            pe.wait_ge(oT_lo_ready, ONE + chunk(NG - 1, NB - 1, 2))
            turn_o(NG - 1, NB - 1, 3)
            pe.wait_ge(y_added, ONE + chunk(NG - 1, NB - 1, 2))
            project_y(NG - 1, NB - 1, 3)


def feed_forward(nc, consts, w13, w2f, x1t, yacc, ln, out):
    with ExitStack() as ctx:
        sb = lambda n, s, d=F32: ctx.enter_context(nc.sbuf_tensor(n, s, d))
        ps = lambda n, s: ctx.enter_context(nc.psum_tensor(n, s, F32))
        sem = lambda n: ctx.enter_context(nc.semaphore(n))
        NW = 3 * HT
        W13, W2 = 2 * KT, HT
        ident = sb("ident2", [P, P])
        stats, mv, var, rstd, spare = ln
        after = spare[:, 0:1]
        turned_x = [sb(f"turned_x{j}", [P, KT, TT * P]) for j in range(2)]
        w_hi, w_lo = sb("fw_hi", [P, NW, 512], F32R), sb("fw_lo", [P, NW, 512], F32R)
        stage = [sb(f"fstage{j}", [P, 512]) for j in range(RING)]
        x_hi, x_lo = sb("fx_hi", [P, KT, 512], F32R), sb("fx_lo", [P, KT, 512], F32R)
        th = [sb(f"th{j}", [P, 512]) for j in range(2)]
        hid = [sb(f"hid{j}", [P, 512]) for j in range(2)]
        h_hi, h_lo = sb("h_hi", [P, HT, 512], F32R), sb("h_lo", [P, HT, 512], F32R)
        bk_gate = [ps(f"bk_gate{j}", [P, 512]) for j in range(2)]
        bk_up = [ps(f"bk_up{j}", [P, 512]) for j in range(2)]
        bk_y = [ps(f"bk_y{j}", [P, 512]) for j in range(TT)]

        id_in = sem("id_in")
        stat_ready, mv_ready, ln_step, normed = sem("stat_ready"), sem("mv_ready"), sem("ln_step"), sem("normed")
        turned, copied = sem("turned"), sem("copied")
        x1_stored = [sem(f"x1_stored{j}") for j in range(2)]
        staged = [sem(f"fstaged{j}") for j in range(RING)]
        st_hi, w_lo_ready, x_lo_ready = sem("fst_hi"), sem("w_lo_ready"), sem("x_lo_ready")
        gate_done, up_done, tanh_ready, act_ready, hid_ready = (sem(n) for n in (
            "fgate_done", "fup_done", "ftanh_ready", "fact_ready", "fhid_ready"))
        h_hi_ready, h_lo_ready = sem("h_hi_ready"), sem("h_lo_ready")
        y_done, y_added = sem("fy_done"), sem("fy_added")
        stat2_ready, mv2_ready, var2_ready, ln2_step, normed2 = (sem(n) for n in (
            "stat2_ready", "mv2_ready", "var2_ready", "ln2_step", "normed2"))
        out_stored = sem("out_stored")
        assert HT == KT == TT == RING == 4 and NTILE == TT * NFS
        LATE = [T // P * (b + 1) - 2 + half for b in range(B) for half in range(2)]
        UNITS = NFS - 1 + 4
        LAST = NHG - 1

        def unit_x(g, s):
            return UNITS * g + (4 + s) if s else UNITS * g + 3

        def unit_w13(g, half):
            return UNITS * g + (1 + half)

        def unit_w2(g):
            return UNITS * g + 4

        def x_tile(g, s, k):
            return KT * NFS * g + KT * s + (k + 1)

        def w_tile(g, w):
            return NW * g + (w + 1)

        def hidden(g, s, h):
            return HT * NFS * g + HT * s + (h + 1)

        block = ctx.enter_context(nc.Block())

        @block.sync
        def _(sp):
            def load_w(g, w):
                src = w13[g, w] if w < W13 else w2f[HT * g + (w - W13)]
                sp.dma_start(stage[w % RING][:, :], src).then_inc(staged[w % RING], 16)

            def load_x(g, s):
                sp.wait_ge(x1_stored[s % 2], 16 * (s // 2 + 1))
                for k in range(KT):
                    if s >= 2:
                        sp.wait_ge(x_lo_ready, x_tile(g, s - 1, k))
                    else:
                        sp.wait_ge(w_lo_ready, w_tile(g, (W13 if s else KT) + k))
                    sp.dma_start(stage[k][:, :], x1t[s, :, k, :]).then_inc(staged[k], 16)

            def next_weights(g):
                for w in range(W13):
                    if w < KT:
                        sp.wait_ge(x_lo_ready, x_tile(g, NFS - 1, w))
                    else:
                        sp.wait_ge(w_lo_ready, w_tile(g + 1, w - KT))
                    load_w(g + 1, w)
                load_x(g + 1, 0)
                for w in range(W13, NW):
                    sp.wait_ge(x_lo_ready, x_tile(g + 1, 0, w - W13))
                    load_w(g + 1, w)

            sp.dma_start(ident[:, :], consts[:, 0:P]).then_inc(id_in, 16)
            for w in range(W13):
                if w >= RING:
                    sp.wait_ge(w_lo_ready, w_tile(0, w - RING))
                load_w(0, w)
            load_x(0, 0)
            for w in range(W13, NW):
                sp.wait_ge(x_lo_ready, x_tile(0, 0, w - W13))
                load_w(0, w)
            with sp.Fori(0, LAST) as g:
                for s in range(1, NFS):
                    load_x(g, s)
                next_weights(g)

            def store(s):
                sp.wait_ge(normed2, TT * (s + 1))
                sp.dma_start(out[:, TT * s:TT * s + TT, :], yacc[:, TT * s:TT * s + TT, :]).then_inc(out_stored, 16)

            for s in range(1, NFS):
                load_x(LAST, s)
                if s >= 2:
                    store(s - 2)
            store(NFS - 2)
            store(NFS - 1)
            sp.wait_ge(out_stored, 16 * NFS)

        @block.scalar
        def _(act):
            def w_high(g, w):
                unit = unit_w2(g) if w >= W13 else unit_w13(g, w // KT)
                act.wait_ge(staged[w % RING], unit * 16)
                act.activation(w_hi[:, w, :], stage[w % RING][:, :], ACT.Copy).then_inc(st_hi, 1)

            def x_high(g, s, unit):
                for k in range(KT):
                    act.wait_ge(staged[k], unit * 16)
                    act.activation(x_hi[:, k, :], stage[k][:, :], ACT.Copy).then_inc(st_hi, 1)

            def turn_out(s):
                if s >= 2:
                    act.wait_ge(x1_stored[s % 2], 16 * (s // 2))
                for j in range(TT):
                    act.wait_ge(turned, TT * s + j + 1)
                    act.activation(turned_x[s % 2][:, :, j * P:(j + 1) * P],
                                   bk_y[j][:, :].rearrange("p (k t) -> p k t", k=KT), ACT.Copy).then_inc(copied, 1)
                act.wait_ge(copied, TT * (s + 1))
                act.dma_start(x1t[s], turned_x[s % 2][:, :, :]).then_inc(x1_stored[s % 2], 16)

            for w in range(KT):
                w_high(0, w)
            turn_out(0)
            for w in range(KT, W13):
                w_high(0, w)
            for s in range(1, 3):
                turn_out(s)
            x_high(0, 0, unit_x(0, 0))
            for s in range(3, NFS):
                turn_out(s)
            for w in range(W13, NW):
                w_high(0, w)

            def hidden_tiles(g, s):
                for h in range(HT):
                    n = hidden(g, s, h)
                    act.wait_ge(gate_done, n)
                    act.activation(th[h % 2][:, :], bk_gate[h % 2][:, :], ACT.Tanh, scale=0.5).then_inc(tanh_ready, 1)
                    act.wait_ge(hid_ready, ONE + n)
                    act.activation(h_hi[:, h, :], hid[h % 2][:, :], ACT.Copy).then_inc(h_hi_ready, 1)
                act.wait_ge(up_done, hidden(g, s, HT - 1))

            def steps_before_last(g):
                with act.Fori(0, NFS - 1) as s:
                    hidden_tiles(g, s)
                    x_high(g, s + 1, UNITS * g + s + 5)
                hidden_tiles(g, NFS - 1)

            with act.Fori(0, LAST) as g:
                steps_before_last(g)
                for w in range(W13):
                    w_high(g + 1, w)
                x_high(g + 1, 0, unit_x(g + 1, 0))
                act.wait_ge(y_done, TT * NFS * g + TT * NFS)
                for w in range(W13, NW):
                    w_high(g + 1, w)
            steps_before_last(LAST)
            for j in range(2):
                act.wait_ge(x1_stored[j], 16 * NFS // 2)

        @block.gpsimd
        def _(pool):
            def x_low(g, s, unit):
                for k in range(KT):
                    pool.wait_ge(st_hi, RING * unit + (k + 1 - RING))
                    pool.tensor_tensor(x_lo[:, k, :], stage[k][:, :], x_hi[:, k, :], ALU.subtract)\
                        .then_inc(x_lo_ready, 1)

            x_low(0, 0, unit_x(0, 0))

            def hidden_tiles(g, s):
                for h in range(HT):
                    n = hidden(g, s, h)
                    pool.wait_ge(h_hi_ready, n)
                    pool.tensor_tensor(h_lo[:, h, :], hid[h % 2][:, :], h_hi[:, h, :], ALU.subtract)\
                        .then_inc(h_lo_ready, 1)

            def steps_before_last(g):
                with pool.Fori(0, NFS - 1) as s:
                    hidden_tiles(g, s)
                    x_low(g, s + 1, UNITS * g + s + 5)
                hidden_tiles(g, NFS - 1)

            with pool.Fori(0, LAST) as g:
                steps_before_last(g)
                x_low(g + 1, 0, unit_x(g + 1, 0))
            steps_before_last(LAST)

        @block.vector
        def _(dve):
            def w_low(g, w):
                unit = unit_w2(g) if w >= W13 else unit_w13(g, w // KT)
                dve.wait_ge(st_hi, RING * unit + (w % RING + 1 - RING))
                dve.tensor_tensor(w_lo[:, w, :], stage[w % RING][:, :], w_hi[:, w, :], ALU.subtract)\
                    .then_inc(w_lo_ready, 1)

            for j, t in enumerate(LATE):
                dve.bn_stats(stats[:, j, :], yacc[:, t, :]).then_inc(stat_ready, 1)
            for j in range(4):
                dve.wait_ge(stat_ready, j + 1)
                dve.bn_aggr(mv[:, j, :], stats[:, j, :]).then_inc(mv_ready, 1)
            dve.wait_ge(mv_ready, 4)
            dve.tensor_scalar(var[:, :], mv[:, :, 1], 1.0, EPS, ALU.mult, ALU.add).then_inc(ln_step, 1)
            dve.wait_ge(ln_step, 1)
            rsqrt(dve, var[:, :], rstd[:, :], spare[:, :], ln_step, 1)
            dve.wait_ge(ln_step, 1 + NEWTON)
            for j, t in enumerate(LATE):
                dve.tensor_scalar(yacc[:, t, :], yacc[:, t, :], mv[:, j, 0:1], rstd[:, j:j + 1],
                                  ALU.subtract, ALU.mult).then_inc(normed, 1)
            for w in range(W13):
                w_low(0, w)
            for w in range(W13, NW):
                w_low(0, w)

            def hidden_tiles(g, s):
                for h in range(HT):
                    n = hidden(g, s, h)
                    dve.wait_ge(tanh_ready, n)
                    dve.scalar_tensor_tensor(out=th[h % 2][:, :], in0=th[h % 2][:, :], scalar=1.0,
                                             in1=bk_gate[h % 2][:, :], op0=ALU.add, op1=ALU.mult)\
                        .then_inc(act_ready, 1)
                    dve.wait_ge(act_ready, n)
                    dve.wait_ge(up_done, n)
                    dve.wait_ge(h_lo_ready, ONE + (n - 2 if h >= 2 else HT * NFS * g + HT * s))
                    dve.tensor_tensor(hid[h % 2][:, :], th[h % 2][:, :], bk_up[h % 2][:, :], ALU.mult)\
                        .then_inc(hid_ready, 1)

            def add_y(g, s):
                for t in range(TT):
                    dve.wait_ge(y_done, TT * NFS * g + TT * s + (t + 1))
                    dve.tensor_tensor(yacc[:, TT * s + t, :], yacc[:, TT * s + t, :], bk_y[t][:, :], ALU.add)\
                        .then_inc(y_added, 1)

            with dve.Fori(0, LAST) as g:
                with dve.Fori(0, NFS - 1) as s:
                    hidden_tiles(g, s)
                    add_y(g, s)
                hidden_tiles(g, NFS - 1)
                for w in range(W13):
                    w_low(g + 1, w)
                add_y(g, NFS - 1)
                for w in range(W13, NW):
                    w_low(g + 1, w)
            with dve.Fori(0, NFS) as s:
                hidden_tiles(LAST, s)
                add_y(LAST, s)
                dve.wait_ge(y_added, ONE + TT * NFS * LAST + TT * s + TT)
                dve.memset(after, 0.0)
                for t in range(TT):
                    dve.bn_stats(stats[:, t, :], yacc[:, TT * s + t, :]).then_inc(stat2_ready, 1)
                dve.wait_ge(stat2_ready, TT * s + TT)
                dve.memset(after, 0.0)
                for t in range(TT):
                    dve.bn_aggr(mv[:, t, :], stats[:, t, :]).then_inc(mv2_ready, 1)
                dve.wait_ge(mv2_ready, TT * s + TT)
                dve.tensor_scalar(var[:, :], mv[:, :, 1], 1.0, EPS, ALU.mult, ALU.add).then_inc(var2_ready, 1)
                dve.wait_ge(var2_ready, s + 1)
                rsqrt(dve, var[:, :], rstd[:, :], spare[:, :], ln2_step, NEWTON * s)
                dve.wait_ge(ln2_step, NEWTON * s + NEWTON)
                for t in range(TT):
                    dve.tensor_scalar(yacc[:, TT * s + t, :], yacc[:, TT * s + t, :], mv[:, t, 0:1], rstd[:, t:t + 1],
                                      ALU.subtract, ALU.mult).then_inc(normed2, 1)

        @block.tensor
        def _(pe):
            for started in (hid_ready, h_lo_ready, y_added):
                pe.sem_inc(started, ONE)
            pe.wait_ge(id_in, 16)
            for n in range(NTILE):
                if n in LATE:
                    pe.wait_ge(normed, LATE.index(n) + 1)
                if n >= TT:
                    pe.wait_ge(copied, n - TT + 1)
                for k in range(KT):
                    mm = pe.transpose(bk_y[n % TT][:, k * P:(k + 1) * P], yacc[:, n, k * P:(k + 1) * P], ident[:, :])
                mm.then_inc(turned, 1)
            with pe.Fori(0, NHG) as g:
                with pe.Fori(0, NFS) as s:
                    pe.wait_ge(w_lo_ready, w_tile(g, W13 - 1))
                    pe.wait_ge(x_lo_ready, x_tile(g, s, KT - 1))
                    for h in range(HT):
                        n = hidden(g, s, h)
                        c = slice(h * P, h * P + P)
                        pe.wait_ge(hid_ready, ONE + (n - 2 if h >= 2 else HT * NFS * g + HT * s))
                        for bank, w0, done in ((bk_gate, 0, gate_done), (bk_up, KT, up_done)):
                            split_product(pe, bank[h % 2][:, :],
                                          [((w_hi[:, w0 + k, c], w_lo[:, w0 + k, c]), (x_hi[:, k, :], x_lo[:, k, :]))
                                           for k in range(KT)]).then_inc(done, 1)
                    pe.wait_ge(copied, NTILE)
                    pe.wait_ge(y_added, ONE + TT * NFS * g + TT * s)
                    pe.wait_ge(w_lo_ready, w_tile(g, NW - 1))
                    for h in range(HT):
                        pe.wait_ge(h_lo_ready, ONE + hidden(g, s, h))
                        for t in range(TT):
                            c = slice(t * P, t * P + P)
                            w = W13 + h
                            pe.matmul(bk_y[t][:, :], h_hi[:, h, c], w_hi[:, w, :], start=(h == 0), stop=False)
                            pe.matmul(bk_y[t][:, :], h_hi[:, h, c], w_lo[:, w, :], start=False, stop=False)
                            mm = pe.matmul(bk_y[t][:, :], h_lo[:, h, c], w_hi[:, w, :], start=False, stop=(h == HT - 1))
                            if h == HT - 1:
                                mm.then_inc(y_done, 1)


def program(nc, consts, x_tok, xt, wt, wo, gw, w13, w2t, w2f, x1t, out):
    with ExitStack() as ctx:
        yacc = ctx.enter_context(nc.sbuf_tensor("yacc", [P, NTILE, D], F32))
        ln = [ctx.enter_context(nc.sbuf_tensor(n, s, F32)) for n, s in (
            ("stats", [P, 4, 6]), ("mv", [P, 4, 2]), ("var", [P, 4]), ("rstd", [P, 4]), ("spare", [P, 4]))]
        out_tok = out.rearrange("b (n p) d -> p (b n) d", p=P)
        hadamard_of_w2(nc, consts, w2t, w2f)
        attention(nc, consts, x_tok.rearrange("b (n p) d -> p (b n) d", p=P), xt, wt, wo, gw,
                  yacc, ln)
        feed_forward(nc, consts, w13, w2f, x1t, yacc, ln, out_tok)


def kernel(**inputs):
    import concourse.bacc as _bacc
    from concourse.bass_utils import run_bass_kernel_spmd as _run

    f32 = np.float32
    x = np.asarray(inputs["L0_attn_hidden_states"])
    wq, wk, wv, wg, ws = (np.asarray(inputs["L0_attn_W" + c]) for c in "qkvgs")
    w1, w2, w3 = (np.asarray(inputs["L0_ffn_W" + c]) for c in "123")

    def tiles(w, n):
        return np.ascontiguousarray(w.reshape(KT, P, n, 512).transpose(0, 2, 1, 3))

    xt = np.ascontiguousarray(x.reshape(B, NB, ST, 2, 2, P).transpose(0, 1, 3, 5, 4, 2)).reshape(B, NB, 2, P, 512)
    groups = []
    for g in range(NG):
        side = np.concatenate([wq[:, g * HG * DK:(g + 1) * HG * DK], wk[:, g * HG * DK:(g + 1) * HG * DK],
                               ws[:, g * HG * M:(g + 1) * HG * M]], axis=1)
        qks = side.reshape(KT, P, QKS).transpose(1, 0, 2).reshape(P, len(QKS_W), 512).transpose(1, 0, 2)
        v, gate = (w[:, g * HG * DV:(g + 1) * HG * DV].reshape(KT, P, 512) for w in (wv, wg))
        groups.append(np.concatenate([qks, v, gate]))
    wt = np.ascontiguousarray(np.stack(groups))
    wo = np.ascontiguousarray(np.asarray(inputs["L0_attn_Wo"]).reshape(NG, HG, P, D))
    gw = np.ascontiguousarray(np.asarray(inputs["L0_attn_g_norm_weight"]).reshape(P, 1))
    w13 = np.ascontiguousarray(np.stack([w.T.reshape(KT, P, NHG, 512).transpose(2, 0, 1, 3) for w in (w1, w3)],
                                        axis=1)).reshape(NHG, 2 * KT, P, 512)
    w2t = np.ascontiguousarray(w2.T.reshape(FF // P, P, 4, P).transpose(2, 1, 0, 3))
    had = np.array([[1.0]], f32)
    while had.shape[0] < P:
        had = np.block([[had, had], [had, -had]])
    consts = np.concatenate([np.eye(P, dtype=f32), np.triu(np.ones((P, P), f32)), had], axis=1).astype(f32)

    nc = _bacc.Bacc("TRN2", target_bir_lowering=False, num_devices=1)
    arrays = {"consts": consts, "x_tok": np.ascontiguousarray(x), "xt": xt, "wt": wt, "wo": wo, "gw": gw,
              "w13": w13, "w2t": w2t}
    aps = [nc.dram_tensor(n, a.shape, mybir.dt.from_np(a.dtype), kind="ExternalInput").ap() for n, a in arrays.items()]
    w2f = nc.dram_tensor("w2f", (FF // P, P, D), F32, kind="Internal").ap()
    x1t = nc.dram_tensor("x1t", (NFS, P, KT, TT * P), F32, kind="Internal").ap()
    out = nc.dram_tensor("out", (B, T, D), F32, kind="ExternalOutput").ap()
    program(nc, *aps, w2f, x1t, out)
    r = _run(nc, [arrays], core_ids=[0])
    return r.results[0]["out"]
```

```python
from contextlib import ExitStack

import numpy as np

import concourse.bass as bass
from concourse import mybir

ALU = mybir.AluOpType
ACT = mybir.ActivationFunctionType
AX_X = mybir.AxisListType.X
F32 = mybir.dt.float32
F32R = mybir.dt.float32r

P = 128
B, T, D = 2, 2048, 512
H, DK, DV, M = 16, 64, 128, 64
FF = 2048
EPS = 1e-5
CLAMP = 32.0
KT = D // P

HG = 4
NG = H // HG
PAIRS = HG // 2
ST = 2 * P
NB = T // ST
NCH = B * T // P
NST = B * T // ST
QC, KC, SC = 0, HG * DK, 2 * HG * DK
QKS = SC + HG * M
QKS_W = range(0, KT * QKS // 512)
V_W = range(QKS_W.stop, QKS_W.stop + KT)
G_W = range(V_W.stop, V_W.stop + KT)
O_W = range(G_W.stop, G_W.stop + HG)
PROJ_TILES, W_TILES = G_W.stop, O_W.stop
W_RING = 3

HT = 4
NHG = FF // (HT * P)
TT = 4
NFS = B * T // (TT * P)
NTILE = B * T // P
A = FF // P
SLICES = D // P
ONE = 1


def split_product(pe, out, terms):
    last = None
    for n, ((a_hi, a_lo), (b_hi, b_lo)) in enumerate(terms):
        pe.matmul(out, a_hi, b_hi, start=(n == 0), stop=False)
        pe.matmul(out, a_hi, b_lo, start=False, stop=False)
        last = pe.matmul(out, a_lo, b_hi, start=False, stop=(n == len(terms) - 1))
    return last


NEWTON = 1 + 3 * 3


def rsqrt(dve, x, y, a, step, base):
    dve.tensor_scalar(y.bitcast(mybir.dt.int32), x.bitcast(mybir.dt.int32), -0.5, float(0x5F375A86),
                      ALU.mult, ALU.add).then_inc(step, 1)
    for k in range(3):
        dve.wait_ge(step, base + (3 * k + 1))
        dve.tensor_tensor(a, y, y, ALU.mult).then_inc(step, 1)
        dve.wait_ge(step, base + (3 * k + 2))
        dve.scalar_tensor_tensor(out=a, in0=a, scalar=-0.5, in1=x, op0=ALU.mult, op1=ALU.mult).then_inc(step, 1)
        dve.wait_ge(step, base + (3 * k + 3))
        dve.scalar_tensor_tensor(out=y, in0=a, scalar=1.5, in1=y, op0=ALU.add, op1=ALU.mult).then_inc(step, 1)


def attention(nc, consts, x_tok, xt, wt, wo, gw, w2t, w2f, yacc, ln):
    with ExitStack() as ctx:
        sb = lambda n, s, d=F32: ctx.enter_context(nc.sbuf_tensor(n, s, d))
        ps = lambda n, s: ctx.enter_context(nc.psum_tensor(n, s, F32))
        sem = lambda n: ctx.enter_context(nc.semaphore(n))

        cst = sb("cst", [P, 4, P])
        ident, causal, had, minus_had = (cst[:, j, :] for j in range(4))
        fly = [[yacc[:, 8 * s + 4 * j:8 * s + 4 * j + 4, :].rearrange("p n (a d) -> p (n a) d", d=P)
                for j in range(2)] for s in range(SLICES)]
        gwc = sb("gwc", [P, 1])
        qks_hi, qks_lo = sb("qks_hi", [P, KT, QKS], F32R), sb("qks_lo", [P, KT, QKS], F32R)
        wv_hi, wv_lo = sb("wv_hi", [P, KT, HG * DV], F32R), sb("wv_lo", [P, KT, HG * DV], F32R)
        wg_hi, wg_lo = sb("wg_hi", [P, KT, HG * DV], F32R), sb("wg_lo", [P, KT, HG * DV], F32R)
        wo_hi, wo_lo = sb("wo_hi", [P, HG, D], F32R), sb("wo_lo", [P, HG, D], F32R)
        w_stage = [sb(f"w_stage{j}", [P, 512]) for j in range(W_RING)]
        x_stage = [sb(f"x_stage{j}", [P, 512]) for j in range(2)]
        x_hi = [sb(f"x_hi{b}", [P, KT, ST], F32R) for b in range(B)]
        x_lo = [sb(f"x_lo{b}", [P, KT, ST], F32R) for b in range(B)]
        qT = [sb(f"qT{b}", [P, PAIRS, ST]) for b in range(B)]
        kT = [sb(f"kT{b}", [P, PAIRS, ST]) for b in range(B)]
        eT = [sb(f"eT{b}", [P, PAIRS, ST]) for b in range(B)]
        zT = [sb(f"zT{b}", [P, PAIRS, ST]) for b in range(B)]
        carry = [sb(f"carry{b}", [P, PAIRS]) for b in range(B)]
        ke = sb("ke", [P, 2, PAIRS, P])
        k_tok, e_tok = ke[:, 0], ke[:, 1]
        rz = sb("rz", [P, HG, M])
        v_tok = sb("v_tok", [P, HG, DV])
        gate = sb("gate", [P, HG * DV])
        qk = sb("qk", [P, 2, PAIRS, P])
        ep = sb("ep", [P, 2, PAIRS, P])
        sm = sb("sm", [P, HG, M])
        pv = sb("pv", [P, HG, M])
        pvT = sb("pvT", [P, PAIRS, P])
        hk = [sb(f"hk{b}", [P, PAIRS, 2 * M]) for b in range(B)]
        hv = [sb(f"hv{b}", [P, PAIRS, 2 * DV]) for b in range(B)]
        ow = sb("ow", [P, HG, DV])
        oT_hi, oT_lo = sb("oT_hi", [P, HG * P], F32R), sb("oT_lo", [P, HG * P], F32R)
        row_max, row_sum, row_rcp = sb("row_max", [P, HG]), sb("row_sum", [P, HG]), sb("row_rcp", [P, HG])
        ssq, t1, t2, t3, fac = (sb(n, [P, HG]) for n in ("ssq", "t1", "t2", "t3", "fac"))

        bk_v = ps("bk_v", [P, 512])
        bk_g = ps("bk_g", [P, 512])
        bk_ab = [ps(f"bk_ab{e}", [P, 2, PAIRS, P]) for e in range(2)]
        bk_ok = ps("bk_ok", [P, 512])
        bk_ov = ps("bk_ov", [P, HG, DV])
        bk_t = ps("bk_t", [P, 512])
        bk_u = ps("bk_u", [P, 512])

        had_bank = [bk_ok[:, :], bk_ab[0][:, :, :, :].rearrange("p j a t -> p (j a t)"),
                    bk_ov[:, :, :].rearrange("p h v -> p (h v)"), bk_t[:, :]]

        cst_in, x_in = sem("cst_in"), sem("x_in")
        slice_in = [sem(f"slice_in{j}") for j in range(SLICES)]
        fly_done, had_done, scaled, w2_stored = sem("fly_done"), sem("had_done"), sem("scaled"), sem("w2_stored")
        w_staged = [sem(f"w_staged{j}") for j in range(W_RING)]
        x_staged = [sem(f"x_staged{j}") for j in range(2)]
        w_hi_ready, w_lo_ready = sem("w_hi_ready"), sem("aw_lo_ready")
        x_hi_ready, x_lo_ready = sem("x_hi_ready"), sem("ax_lo_ready")
        s_done, q_done, k_done = sem("s_done"), sem("q_done"), sem("k_done")
        clipped, e_ready, scanned, z_ready = sem("clipped"), sem("e_ready"), sem("scanned"), sem("z_ready")
        carried = sem("carried")
        q_ready, k_ready = sem("q_ready"), sem("k_ready")
        ke_done, ke_ready = sem("ke_done"), sem("ke_ready")
        qk_done, qk_ready = sem("qk_done"), sem("qk_ready")
        rz_done, rz_ready = sem("rz_done"), sem("rz_ready")
        v_done, v_ready = sem("v_done"), sem("v_ready")
        ok_done, okz_ready, max_ready, sub_ready = sem("ok_done"), sem("okz_ready"), sem("max_ready"), sem("sub_ready")
        exp_ready, sum_ready, pv_ready = sem("exp_ready"), sem("sum_ready"), sem("pv_ready")
        rcp_ready = sem("rcp_ready")
        hk_done, hk_ready = sem("hk_done"), sem("hk_ready")
        g_done, tanh_ready, gate_ready = sem("g_done"), sem("tanh_ready"), sem("gate_ready")
        pvT_done, pvT_ready = sem("pvT_done"), sem("pvT_ready")
        ep_done, ep_ready = sem("ep_done"), sem("ep_ready")
        ov_done, sq_ready, ssq_ready = sem("ov_done"), sem("sq_ready"), sem("ssq_ready")
        t1_ready, t2_ready, t3_ready, fac_ready = sem("t1_ready"), sem("t2_ready"), sem("t3_ready"), sem("fac_ready")
        ow_ready = sem("ow_ready")
        hv_done, hv_ready = sem("hv_done"), sem("hv_ready")
        oT_done, oT_hi_ready, oT_lo_ready = sem("oT_done"), sem("oT_hi_ready"), sem("oT_lo_ready")
        y_done, y_added = sem("y_done"), sem("y_added")
        zeroed, newton = sem("zeroed"), sem("newton")
        ln_stat, ln_mv, ln_var, ln_newton = sem("ln_stat"), sem("ln_mv"), sem("ln_var"), sem("ln_newton")

        def every_step(eng, one_step):
            one_step(0, 0)
            with eng.Fori(0, NG - 1) as g:
                with eng.Fori(1, NB - 1) as i:
                    one_step(g, i)
                one_step(g, NB - 1)
                one_step(g + 1, 0)
            with eng.Fori(1, NB - 1) as i:
                one_step(NG - 1, i)
            one_step(NG - 1, NB - 1)

        def is_at(value, at):
            return isinstance(value, int) and value == at

        def parts(w):
            if w in QKS_W:
                c = slice(512 * w, 512 * w + 512)
                return [t[:, :, :].rearrange("p k c -> p (k c)")[:, c] for t in (qks_hi, qks_lo)]
            hi, lo, first = ((wv_hi, wv_lo, V_W.start) if w in V_W else
                             (wg_hi, wg_lo, G_W.start) if w in G_W else (wo_hi, wo_lo, O_W.start))
            return [hi[:, w - first, :], lo[:, w - first, :]]

        def chunk(g, i, r):
            return NCH * g + 4 * i + (r + 1)

        def super_(g, i, b):
            return NST * g + 2 * i + (b + 1)

        def x_tile(g, i, b, half):
            return 2 * NST * g + 4 * i + (2 * b + half + 1)

        def w_tile(g, w):
            return W_TILES * g + (w + 1)

        block = ctx.enter_context(nc.Block())

        @block.sync
        def _(sp):
            sp.dma_start(cst[:, :, :], consts.rearrange("p (a c) -> p a c", a=4)).then_inc(cst_in, 16)
            sp.dma_start(gwc[:, :], gw).then_inc(cst_in, 16)

            def load_w(g, w):
                sp.wait_ge(w_lo_ready, ONE + W_TILES * g + max(w + 1 - W_RING, 0))
                src = wt[g, w] if w < PROJ_TILES else wo[g, w - PROJ_TILES]
                sp.dma_start(w_stage[w % W_RING][:, :], src).then_inc(w_staged[w % W_RING], 16)

            def load_x(g, i, b):
                sp.wait_ge(x_lo_ready, ONE + x_tile(g, i, b, 0) - 1)
                for half in range(2):
                    sp.dma_start(x_stage[half][:, :], xt[b, i, half]).then_inc(x_staged[half], 16)

            with sp.Fori(0, NG) as g:
                for w in QKS_W[:3]:
                    load_w(g, w)
                load_x(g, 0, 0)
                for w in [*QKS_W[3:], *V_W, *G_W]:
                    load_w(g, w)
                load_x(g, 0, 1)
                for w in O_W[:3]:
                    load_w(g, w)
                load_x(g, 1, 0)
                for w in O_W[3:]:
                    load_w(g, w)
                load_x(g, 1, 1)
                with sp.Fori(2, NB) as i:
                    for b in range(B):
                        load_x(g, i, b)

        @block.gpsimd
        def _(pool):
            for s in range(SLICES):
                pool.dma_start(fly[s][0], w2t[s]).then_inc(slice_in[s], 16)

            def w_low(*tiles):
                for w in tiles:
                    pool.wait_ge(w_hi_ready, w_tile(0, w))
                    pool.tensor_tensor(parts(w)[1], w_stage[w % W_RING][:, :], parts(w)[0], ALU.subtract)\
                        .then_inc(w_lo_ready, 1)

            def x_low(i, b):
                for half in range(2):
                    pool.wait_ge(x_hi_ready, x_tile(0, i, b, half))
                    dst = slice(half * 2, half * 2 + 2)
                    pool.tensor_tensor(x_lo[b][:, dst, :].rearrange("p k t -> p (k t)"), x_stage[half][:, :],
                                       x_hi[b][:, dst, :].rearrange("p k t -> p (k t)"), ALU.subtract)\
                        .then_inc(x_lo_ready, 1)

            w_low(*QKS_W)
            x_low(0, 0)
            w_low(*V_W, *G_W[:2])
            x_low(0, 1)
            pool.wait_ge(w2_stored, 16 * SLICES)
            for c in range(4):
                pool.dma_start(yacc[:, 8 * c:8 * c + 8, :], x_tok[:, 8 * c:8 * c + 8, :]).then_inc(x_in, 16)

            with pool.Fori(1, NG * NB) as i:
                for b in range(B):
                    x_low(i, b)

        @block.scalar
        def _(act):
            act.wait_ge(cst_in, 32)

            def x_high(g, i, b):
                for half in range(2):
                    act.wait_ge(x_staged[half], super_(g, i, b) * 16)
                    act.activation(x_hi[b][:, half * 2:half * 2 + 2, :].rearrange("p k t -> p (k t)"),
                                   x_stage[half][:, :], ACT.Copy).then_inc(x_hi_ready, 1)

            def w_high(g, *tiles):
                for w in tiles:
                    act.wait_ge(w_staged[w % W_RING], (W_TILES // W_RING * g + (w // W_RING + 1)) * 16)
                    if w in O_W:
                        act.activation(parts(w)[0], w_stage[w % W_RING][:, :], ACT.Copy, scale=gwc[:, 0:1])\
                            .then_inc(w_hi_ready, 1)
                    else:
                        act.activation(parts(w)[0], w_stage[w % W_RING][:, :], ACT.Copy).then_inc(w_hi_ready, 1)

            def exp_s(g, i, b):
                act.wait_ge(clipped, super_(g, i, b))
                act.activation(eT[b][:, :, :], eT[b][:, :, :], ACT.Exp).then_inc(e_ready, 1)

            def q_copy(g, i, b):
                act.wait_ge(q_done, super_(g, i, b))
                act.activation(qT[b][:, :, :], bk_g[:, :].rearrange("p (a t) -> p a t", a=PAIRS), ACT.Copy)\
                    .then_inc(q_ready, 1)

            def k_copy(g, i, b):
                act.wait_ge(k_done, super_(g, i, b))
                act.activation(kT[b][:, :, :], bk_v[:, :].rearrange("p (a t) -> p a t", a=PAIRS), ACT.Copy)\
                    .then_inc(k_ready, 1)

            def square_o(g, i, r):
                act.wait_ge(ov_done, chunk(g, i, r))
                act.activation(ow[:, :, :], bk_ov[:, :, :], ACT.Square).then_inc(sq_ready, 1)

            def o_high(g, i, r):
                act.wait_ge(oT_done, chunk(g, i, r))
                act.activation(oT_hi[:, :], bk_t[:, :], ACT.Copy).then_inc(oT_hi_ready, 1)

            def scale_w2(s):
                for j in range(4):
                    act.wait_ge(had_done, 4 * s + j + 1)
                    act.activation(fly[s][0][:, 4 * j:4 * j + 4, :].rearrange("p a d -> p (a d)"), had_bank[j],
                                   ACT.Copy, scale=0.5 * float(np.float32(1.0 / np.sqrt(FF)))).then_inc(scaled, 1)
                act.wait_ge(scaled, 4 * s + 4)
                act.dma_start(w2f[:, :, s * P:(s + 1) * P].rearrange("a p d -> p a d"), fly[s][0])\
                    .then_inc(w2_stored, 16)

            w_high(0, *QKS_W)
            x_high(0, 0, 0)
            scale_w2(0)
            w_high(0, *V_W)
            scale_w2(1)
            w_high(0, *G_W[:2])
            scale_w2(2)
            exp_s(0, 0, 0)
            scale_w2(3)
            q_copy(0, 0, 0)
            k_copy(0, 0, 0)

            def one_step(g, i):
                start, end, last = is_at(i, 0), is_at(i, NB - 1), is_at(g, NG - 1)
                for r in range(4):
                    b = r // 2
                    n = chunk(g, i, r)
                    nxt = (i, 1) if r < 2 else (i + 1, 0)
                    more = not (end and last and r >= 2)
                    reload = end and r >= 2 and not last
                    if not (start and is_at(g, 0) and r < 2):
                        o_high(g, i, r - 2)
                    if start and r == 2:
                        if not is_at(g, 0):
                            act.wait_ge(y_done, ONE + NCH * g)
                        w_high(g, *O_W[:2])
                    if not (start and is_at(g, 0) and r == 0):
                        square_o(g, i, r - 1)
                    if start and r == 2:
                        w_high(g, *O_W[2:])
                    if reload and r == 2:
                        w_high(g + 1, *QKS_W[:2])
                    if r % 2 == 0 and more:
                        act.wait_ge(g_done, ONE + n - 1)
                        x_high(g, *nxt)
                    if reload and r == 2:
                        w_high(g + 1, QKS_W[2])
                    if start and r == 0:
                        w_high(g, *G_W[2:])
                    act.wait_ge(ke_done, n)
                    act.activation(ke[:, :, :, :], bk_t[:, :].rearrange("p (a c t) -> p a c t", a=2, c=2),
                                   ACT.Copy).then_inc(ke_ready, 1)
                    if reload and r == 2:
                        w_high(g + 1, QKS_W[3])
                    act.wait_ge(rz_done, n)
                    act.activation(rz[:, :, :], bk_u[:, 0:HG * M].rearrange("p (h m) -> p h m", h=HG),
                                   ACT.Copy).then_inc(rz_ready, 1)
                    if reload and r == 2:
                        w_high(g + 1, QKS_W[4])
                    act.wait_ge(v_done, n)
                    act.activation(v_tok[:, :, :], bk_v[:, :].rearrange("p (h v) -> p h v", h=HG),
                                   ACT.Copy).then_inc(v_ready, 1)
                    if reload and r == 2:
                        w_high(g + 1, QKS_W[5])
                    act.wait_ge(sub_ready, n)
                    act.activation(sm[:, :, :], sm[:, :, :], ACT.Exp, scale=DK ** -0.5).then_inc(exp_ready, 1)
                    if reload and r == 3:
                        w_high(g + 1, *V_W[:2])
                    act.wait_ge(g_done, ONE + n)
                    act.wait_ge(ow_ready, ONE + HG * (n - 1))
                    act.activation(gate[:, :], bk_g[:, :], ACT.Tanh, scale=0.5).then_inc(tanh_ready, 1)
                    if reload and r == 3:
                        w_high(g + 1, *V_W[2:])
                    act.wait_ge(pvT_done, n)
                    act.activation(pvT[:, :, :], bk_ok[:, 256:512].rearrange("p (a t) -> p a t", a=PAIRS),
                                   ACT.Copy).then_inc(pvT_ready, 1)
                    if reload and r == 3:
                        w_high(g + 1, *G_W[:2])
                    if more:
                        if r % 2 == 0:
                            exp_s(g, *nxt)
                        else:
                            q_copy(g, *nxt)
                            k_copy(g, *nxt)

            every_step(act, one_step)
            o_high(NG - 1, NB - 1, 2)
            square_o(NG - 1, NB - 1, 3)
            o_high(NG - 1, NB - 1, 3)

        @block.vector
        def _(dve):
            dve.wait_ge(cst_in, 32)

            def butterflies(s):
                for j in range(3):
                    dve.wait_ge(*((fly_done, 6 * s + 2 * j) if j else (slice_in[s], 16)))
                    src, dst = (fly[s][k % 2].rearrange("p (n t h) d -> p n t h d", t=2, h=2 ** j) for k in (j, j + 1))
                    a, b = src[:, :, 0], src[:, :, 1]
                    dve.tensor_tensor(dst[:, :, 0], a, b, ALU.add).then_inc(fly_done, 1)
                    dve.tensor_tensor(dst[:, :, 1], a, b, ALU.subtract).then_inc(fly_done, 1)

            def clip_s(g, i, b):
                dve.wait_ge(s_done, super_(g, i, b))
                dve.tensor_scalar(eT[b][:, :, :], bk_g[:, :].rearrange("p (a t) -> p a t", a=PAIRS),
                                  CLAMP, -CLAMP, ALU.min, ALU.max).then_inc(clipped, 1)

            def scan_e(g, i, b):
                dve.wait_ge(e_ready, super_(g, i, b))
                for a in range(PAIRS):
                    dve.tensor_tensor_scan(zT[b][:, a, :], eT[b][:, a, :], eT[b][:, a, :], carry[b][:, a:a + 1],
                                           ALU.add, ALU.max).then_inc(scanned, 1)
                dve.wait_ge(scanned, 2 * super_(g, i, b))
                dve.tensor_copy(carry[b][:, :], zT[b][:, :, ST - 1]).then_inc(carried, 1)

            def invert_z(g, i, b):
                dve.wait_ge(carried, super_(g, i, b))
                dve.reciprocal(zT[b][:, :, :], zT[b][:, :, :]).then_inc(z_ready, 1)

            def update_hv(g, i, r):
                b = r % 4 // 2
                dve.wait_ge(hv_done, chunk(g, i, r))
                upd = bk_u[:, :].rearrange("p (a c) -> p a c", a=PAIRS)
                for e in range(2):
                    rows, cols = slice(64 * e, 64 * e + 64), slice(DV * e, DV * e + DV)
                    dve.tensor_tensor(hv[b][rows, :, cols], hv[b][rows, :, cols], upd[rows, :, cols], ALU.add)\
                        .then_inc(hv_ready, 1)

            def update_hk(g, i, r):
                b = r // 2
                dve.wait_ge(hk_done, chunk(g, i, r))
                upd = bk_u[:, 256:512].rearrange("p (a c) -> p a c", a=PAIRS)
                for e in range(2):
                    rows, cols = slice(64 * e, 64 * e + 64), slice(M * e, M * e + M)
                    dve.tensor_tensor(hk[b][rows, :, cols], hk[b][rows, :, cols], upd[rows, :, cols], ALU.add)\
                        .then_inc(hk_ready, 1)

            def factor_o(g, i, r):
                n = chunk(g, i, r)
                dve.wait_ge(sq_ready, n)
                dve.tensor_reduce(ssq[:, :], ow[:, :, :], AX_X, ALU.add).then_inc(ssq_ready, 1)
                dve.wait_ge(ssq_ready, n)
                dve.wait_ge(rcp_ready, n)
                dve.tensor_tensor(t1[:, :], ssq[:, :], row_rcp[:, :], ALU.mult).then_inc(t1_ready, 1)
                dve.wait_ge(t1_ready, n)
                dve.tensor_tensor(t2[:, :], t1[:, :], row_rcp[:, :], ALU.mult).then_inc(t2_ready, 1)
                dve.wait_ge(t2_ready, n)
                dve.tensor_scalar(t1[:, :], t2[:, :], 1.0, DV * EPS, ALU.mult, ALU.add).then_inc(t3_ready, 1)
                dve.wait_ge(t3_ready, n)
                rsqrt(dve, t1[:, :], t3[:, :], t2[:, :], newton, NEWTON * (n - 1))
                dve.wait_ge(newton, NEWTON * n)
                dve.scalar_tensor_tensor(out=fac[:, :], in0=t3[:, :], scalar=0.5 * DV ** 0.5, in1=row_rcp[:, :],
                                         op0=ALU.mult, op1=ALU.mult).then_inc(fac_ready, 1)

            def gate_o(g, i, r):
                n = chunk(g, i, r)
                dve.wait_ge(fac_ready, n)
                dve.wait_ge(gate_ready, ONE + n)
                for h in range(HG):
                    dve.scalar_tensor_tensor(out=ow[:, h, :], in0=bk_ov[:, h, :], scalar=fac[:, h:h + 1],
                                             in1=gate[:, h * DV:(h + 1) * DV], op0=ALU.mult, op1=ALU.mult)\
                        .then_inc(ow_ready, 1)

            def o_low(g, i, r):
                dve.wait_ge(oT_hi_ready, chunk(g, i, r))
                dve.tensor_tensor(oT_lo[:, :], bk_t[:, :], oT_hi[:, :], ALU.subtract).then_inc(oT_lo_ready, 1)

            def add_y(g, i, r):
                before = (NB if is_at(i, 0) else i) - 1 if r < 0 else i
                at = T // P * (r % 4 // 2) + 2 * before + r % 2
                dve.wait_ge(y_done, ONE + chunk(g, i, r))
                dve.tensor_tensor(yacc[:, at, :], yacc[:, at, :], bk_v[:, :], ALU.add).then_inc(y_added, 1)

            stats, mv, var, rstd, spare = ln
            after = spare[:, 0:1]

            def norm_rows(s, r, part):
                tiles = [T // P * part + 2 * s + half for half in range(2)]
                if r == 1:
                    dve.wait_ge(y_added, ONE + chunk(NG - 1, s, 1 + 2 * part))
                    if not isinstance(s, int):
                        dve.memset(after, 0.0)
                    for j, t in enumerate(tiles, 2 * part):
                        dve.bn_stats(stats[:, j, :], yacc[:, t, :]).then_inc(ln_stat, 1)
                if r == 2 and part == 0:
                    dve.wait_ge(ln_stat, 4 * s + 4)
                    if not isinstance(s, int):
                        dve.memset(after, 0.0)
                    for j in range(4):
                        dve.bn_aggr(mv[:, j, :], stats[:, j, :]).then_inc(ln_mv, 1)
                    dve.wait_ge(ln_mv, 4 * s + 4)
                    dve.tensor_scalar(var[:, :], mv[:, :, 1], 1.0, EPS, ALU.mult, ALU.add).then_inc(ln_var, 1)
                if r == 2 and part == 1:
                    dve.wait_ge(ln_var, s + 1)
                    rsqrt(dve, var[:, :], rstd[:, :], spare[:, :], ln_newton, NEWTON * s)
                if r == 3:
                    dve.wait_ge(ln_newton, NEWTON * s + NEWTON)
                    for j, t in enumerate(tiles, 2 * part):
                        dve.tensor_scalar(yacc[:, t, :], yacc[:, t, :], mv[:, j, 0:1], rstd[:, j:j + 1],
                                          ALU.subtract, ALU.mult)

            def w_low(g, *tiles):
                for w in tiles:
                    hi, lo = parts(w)
                    dve.wait_ge(w_hi_ready, w_tile(g, w))
                    if w in O_W:
                        dve.scalar_tensor_tensor(out=lo, in0=w_stage[w % W_RING][:, :], scalar=gwc[:, 0:1], in1=hi,
                                                 op0=ALU.mult, op1=ALU.subtract).then_inc(w_lo_ready, 1)
                    else:
                        dve.tensor_tensor(lo, w_stage[w % W_RING][:, :], hi, ALU.subtract).then_inc(w_lo_ready, 1)

            def zero_states(b):
                for t in (hk[b][:, :, :], hv[b][:, :, :], carry[b][:, :]):
                    dve.memset(t, 0.0).then_inc(zeroed, 1)

            zero_states(0)
            zero_states(1)
            for s in range(3):
                butterflies(s)
            clip_s(0, 0, 0)
            butterflies(3)
            dve.wait_ge(zeroed, 6)
            scan_e(0, 0, 0)
            invert_z(0, 0, 0)

            def one_step(g, i):
                start, end, last = is_at(i, 0), is_at(i, NB - 1), is_at(g, NG - 1)
                for r in range(4):
                    b = r // 2
                    n = chunk(g, i, r)
                    nxt = (i, 1) if r < 2 else (i + 1, 0)
                    first = start and is_at(g, 0) and r == 0
                    behind = start and is_at(g, 0) and r < 2
                    more = not (end and last and r >= 2)
                    reload = end and r >= 2 and not last
                    if not behind:
                        o_low(g, i, r - 2)
                    if start and r == 2:
                        w_low(g, O_W[0])
                    if not first:
                        update_hv(g, i, r - 1)
                    if start and r == 2:
                        w_low(g, O_W[1])
                    if reload and r == 2:
                        w_low(g + 1, QKS_W[0])
                    dve.wait_ge(qk_done, n)
                    mask = causal.unsqueeze(1).broadcast_to([P, PAIRS, P])
                    for e in range(2):
                        dve.tensor_tensor(qk[:, e], bk_ab[e][:, 0], mask, ALU.mult).then_inc(qk_ready, 1)
                    if start and r == 2:
                        w_low(g, *O_W[2:])
                    if start and r == 0:
                        if first:
                            dve.wait_ge(w_lo_ready, ONE + w_tile(0, G_W[1]))
                        w_low(g, *G_W[2:])
                    if reload and r == 2:
                        w_low(g + 1, QKS_W[1])
                    if (reload and r == 2) or (start and r == 0 and not first):
                        dve.wait_ge(hv_ready, ONE + 2 * n - 2)
                        dve.wait_ge(hk_ready, ONE + 2 * n - 2)
                        zero_states(0 if reload else 1)
                    if not first:
                        factor_o(g, i, r - 1)
                    if reload and r == 2:
                        w_low(g + 1, QKS_W[2])
                    if r % 2 == 1 and more:
                        if (start and r == 1) or (end and r == 3):
                            dve.wait_ge(zeroed, 6 * g + (6 if r == 1 else 9))
                        scan_e(g, *nxt)
                    dve.wait_ge(ok_done, n)
                    dve.wait_ge(rz_ready, n)
                    dve.tensor_tensor(sm[:, :, :], bk_ok[:, 0:HG * M].rearrange("p (h m) -> p h m", h=HG),
                                      rz[:, :, :], ALU.mult).then_inc(okz_ready, 1)
                    dve.wait_ge(okz_ready, n)
                    dve.tensor_reduce(row_max[:, :], sm[:, :, :], AX_X, ALU.max).then_inc(max_ready, 1)
                    dve.wait_ge(max_ready, n)
                    dve.tensor_tensor(sm[:, :, :], sm[:, :, :], row_max[:, :].unsqueeze(2).broadcast_to([P, HG, M]),
                                      ALU.subtract).then_inc(sub_ready, 1)
                    if reload and r == 2:
                        w_low(g + 1, QKS_W[3])
                    if not first:
                        gate_o(g, i, r - 1)
                    update_hk(g, i, r)
                    if reload and r == 2:
                        w_low(g + 1, QKS_W[4])
                    if reload and r == 3:
                        w_low(g + 1, V_W[0])
                    dve.wait_ge(exp_ready, n)
                    dve.tensor_tensor(pv[:, :, :], sm[:, :, :], rz[:, :, :], ALU.mult).then_inc(pv_ready, 1)
                    dve.tensor_reduce(row_sum[:, :], sm[:, :, :], AX_X, ALU.add).then_inc(sum_ready, 1)
                    if reload and r == 2:
                        w_low(g + 1, QKS_W[5])
                    if reload and r == 3:
                        w_low(g + 1, V_W[1])
                    dve.wait_ge(sum_ready, n)
                    dve.reciprocal(row_rcp[:, :], row_sum[:, :]).then_inc(rcp_ready, 1)
                    dve.wait_ge(tanh_ready, n)
                    dve.scalar_tensor_tensor(out=gate[:, :], in0=gate[:, :], scalar=1.0, in1=bk_g[:, :],
                                             op0=ALU.add, op1=ALU.mult).then_inc(gate_ready, 1)
                    if last and r:
                        norm_rows(i - 1, r, 0)
                    if start and is_at(g, 0) and r == 2:
                        dve.wait_ge(x_in, 64)
                    if not behind:
                        add_y(g, i, r - 2)
                    if reload and r == 3:
                        w_low(g + 1, *V_W[2:])
                    if r % 2 == 1 and more:
                        invert_z(g, *nxt)
                    dve.wait_ge(ep_done, n)
                    for e in range(2):
                        dve.tensor_tensor(ep[:, e], bk_ab[e][:, 1], mask, ALU.mult).then_inc(ep_ready, 1)
                    if reload and r == 3:
                        w_low(g + 1, *G_W[:2])
                    if r % 2 == 0 and more:
                        clip_s(g, *nxt)
                    if last and r:
                        norm_rows(i - 1, r, 1)

            every_step(dve, one_step)
            o_low(NG - 1, NB - 1, 2)
            update_hv(NG - 1, NB - 1, 3)
            factor_o(NG - 1, NB - 1, 3)
            gate_o(NG - 1, NB - 1, 3)
            add_y(NG - 1, NB - 1, 2)
            o_low(NG - 1, NB - 1, 3)
            add_y(NG - 1, NB - 1, 3)

        @block.tensor
        def _(pe):
            for started in (w_lo_ready, x_lo_ready, g_done, y_done, gate_ready, y_added, oT_lo_ready, ep_ready, hv_ready, hk_ready,
                            pvT_ready, ow_ready):
                pe.sem_inc(started, ONE)
            pe.wait_ge(cst_in, 32)

            def transposed(out, b, col, a):
                c = slice(col + a * P, col + a * P + P)
                return split_product(pe, out[:, a * ST:(a + 1) * ST],
                                     [((qks_hi[:, k, c], qks_lo[:, k, c]), (x_hi[b][:, k, :], x_lo[b][:, k, :]))
                                      for k in range(KT)])

            def by_token(out, b, half, hi, lo):
                t = slice(half * P, half * P + P)
                return split_product(pe, out[:, :],
                                     [((x_hi[b][:, k, t], x_lo[b][:, k, t]), (hi[:, k, :], lo[:, k, :]))
                                      for k in range(KT)])

            def values(g, i, r):
                b = r % 4 // 2
                n = chunk(g, i, r)
                pe.wait_ge(ep_ready, ONE + 2 * n)
                pe.wait_ge(hv_ready, ONE + 2 * n - 2)
                pe.wait_ge(ow_ready, ONE + 4 * n - 4)
                pe.wait_ge(v_ready, n)
                for a in range(PAIRS):
                    pe.matmul(bk_ov[:, 2 * a:2 * a + 2, :], pvT[:, a, :], hv[b][:, a, :].rearrange("p (e v) -> p e v", e=2),
                              start=True, stop=False)
                    for e in range(2):
                        mm = pe.matmul(bk_ov[:, 2 * a + e, :], ep[:, e, a, :], v_tok[:, 2 * a + e, :],
                                       start=False, stop=(e == 1))
                mm.then_inc(ov_done, 1)
                pe.wait_ge(hk_ready, ONE + 2 * n)
                for a in range(PAIRS):
                    mm = pe.matmul(bk_u[:, 256 * a:256 * a + 256], e_tok[:, a, :],
                                   v_tok[:, 2 * a:2 * a + 2, :].rearrange("p h v -> p (h v)"), start=True, stop=True)
                mm.then_inc(hv_done, 1)

            def turn_o(g, i, r):
                n = chunk(g, i, r)
                pe.wait_ge(ow_ready, ONE + 4 * n)
                for h in range(HG):
                    mm = pe.transpose(bk_t[:, P * h:P * h + P], ow[:, h, :], ident)
                mm.then_inc(oT_done, 1)

            def project_y(g, i, r):
                pe.wait_ge(oT_lo_ready, ONE + chunk(g, i, r))
                split_product(pe, bk_v[:, :], [((oT_hi[:, P * h:P * h + P], oT_lo[:, P * h:P * h + P]),
                                                (wo_hi[:, h, :], wo_lo[:, h, :])) for h in range(HG)])\
                    .then_inc(y_done, 1)

            def hadamard(s):
                pe.wait_ge(fly_done, 6 * s + 6)
                for j in range(4):
                    if s:
                        pe.wait_ge(scaled, 4 * (s - 1) + j + 1)
                    low, high = (fly[s][1][:, 4 * k:4 * k + 4, :].rearrange("p a d -> p (a d)")
                                 for k in (j % 2, j % 2 + 2))
                    pe.matmul(had_bank[j], had, low, start=True, stop=False)
                    pe.matmul(had_bank[j], had if j < 2 else minus_had, high, start=False, stop=True)\
                        .then_inc(had_done, 1)

            hadamard(0)
            hadamard(1)
            pe.wait_ge(w_lo_ready, ONE + w_tile(0, QKS_W[-1]))
            pe.wait_ge(x_lo_ready, ONE + x_tile(0, 0, 0, 1))
            for a in range(PAIRS):
                mm = transposed(bk_g, 0, SC, a)
            mm.then_inc(s_done, 1)
            hadamard(2)
            for a in range(PAIRS):
                mm = transposed(bk_v, 0, KC, a)
            mm.then_inc(k_done, 1)
            hadamard(3)
            pe.wait_ge(clipped, 1)
            for a in range(PAIRS):
                mm = transposed(bk_g, 0, QC, a)
            mm.then_inc(q_done, 1)
            pe.wait_ge(scaled, 4 * SLICES)

            def one_step(g, i):
                start, end, last = is_at(i, 0), is_at(i, NB - 1), is_at(g, NG - 1)
                for r in range(4):
                    b, half = r // 2, r % 2
                    n = chunk(g, i, r)
                    nxt = (i, 1) if r < 2 else (i + 1, 0)
                    nb = 1 - b
                    m = super_(g, *nxt)
                    first = start and is_at(g, 0) and r == 0
                    more = not (end and last and r >= 2)
                    t = slice(half * P, half * P + P)
                    behind = start and is_at(g, 0) and r < 2
                    if not behind:
                        pe.wait_ge(ke_ready, n - 1)
                        turn_o(g, i, r - 2)
                    if not first:
                        values(g, i, r - 1)
                    if half == 0:
                        pe.wait_ge(k_ready, super_(g, i, b))
                        pe.wait_ge(e_ready, super_(g, i, b))
                        pe.wait_ge(q_ready, super_(g, i, b))
                        pe.wait_ge(z_ready, super_(g, i, b))
                    if not behind:
                        pe.wait_ge(oT_lo_ready, ONE + n - 2)
                    elif r == 1:
                        pe.wait_ge(ke_ready, n - 1)
                    for a in range(PAIRS):
                        pe.transpose(bk_t[:, P * a:P * a + P], kT[b][:, a, t], ident)
                    for a in range(PAIRS):
                        mm = pe.transpose(bk_t[:, 256 + P * a:256 + P * a + P], eT[b][:, a, t], ident)
                    mm.then_inc(ke_done, 1)
                    pe.wait_ge(ep_ready, ONE + 2 * n - 2)
                    for a in range(PAIRS):
                        for e in range(2):
                            rows = slice(64 * e, 64 * e + 64)
                            mm = pe.matmul(bk_ab[e][:, 0, a, :], kT[b][rows, a, t], qT[b][rows, a, t],
                                           start=True, stop=True)
                    mm.then_inc(qk_done, 1)
                    pe.wait_ge(hv_ready, ONE + 2 * n - 2)
                    for a in range(PAIRS):
                        mm = pe.transpose(bk_u[:, P * a:P * a + P], zT[b][:, a, t], ident)
                    mm.then_inc(rz_done, 1)
                    if half == 0:
                        pe.wait_ge(k_ready, super_(g, i, b))
                    elif behind:
                        pe.wait_ge(v_ready, n - 1)
                    else:
                        pe.wait_ge(y_added, ONE + n - 3)
                    if start and r == 0:
                        pe.wait_ge(w_lo_ready, ONE + w_tile(g, V_W[-1]))
                    by_token(bk_v, b, half, wv_hi, wv_lo).then_inc(v_done, 1)
                    pe.wait_ge(qk_ready, 2 * n)
                    pe.wait_ge(ke_ready, n)
                    pe.wait_ge(hk_ready, ONE + 2 * n - 2)
                    pe.wait_ge(pvT_ready, ONE + n - 1)
                    if start and half == 0:
                        pe.wait_ge(zeroed, 6 * g + 3 * (b + 1))
                    for a in range(PAIRS):
                        pe.matmul(bk_ok[:, P * a:P * a + P], qT[b][:, a, t], hk[b][:, a, :], start=True, stop=False)
                        for e in range(2):
                            o = P * a + M * e
                            mm = pe.matmul(bk_ok[:, o:o + M], qk[:, e, a, :], e_tok[:, a, M * e:M * e + M],
                                           start=False, stop=(e == 1))
                    mm.then_inc(ok_done, 1)
                    pe.wait_ge(rz_ready, n)
                    for a in range(PAIRS):
                        mm = pe.matmul(bk_u[:, 256 + P * a:256 + P * a + P], k_tok[:, a, :], e_tok[:, a, :],
                                       start=True, stop=True)
                    mm.then_inc(hk_done, 1)
                    if half == 0:
                        pe.wait_ge(q_ready, super_(g, i, b))
                    elif more:
                        pe.wait_ge(clipped, m)
                    else:
                        pe.wait_ge(gate_ready, ONE + n - 1)
                    if start and r == 0:
                        pe.wait_ge(w_lo_ready, ONE + w_tile(g, G_W[-1]))
                    by_token(bk_g, b, half, wg_hi, wg_lo).then_inc(g_done, 1)
                    pe.wait_ge(v_ready, n)
                    if start and r == 2:
                        pe.wait_ge(w_lo_ready, ONE + w_tile(g, O_W[-1]))
                    if not behind:
                        project_y(g, i, r - 2)
                    pe.wait_ge(pv_ready, n)
                    for a in range(PAIRS):
                        mm = pe.transpose(bk_ok[:, 256 + P * a:256 + P * a + P],
                                          pv[:, 2 * a:2 * a + 2, :].rearrange("p h m -> p (h m)"), ident)
                    mm.then_inc(pvT_done, 1)
                    if more:
                        pe.wait_ge(gate_ready, ONE + n)
                        if half == 0:
                            pe.wait_ge(x_lo_ready, ONE + x_tile(g, *nxt, 1))
                            if end and r == 2:
                                pe.wait_ge(w_lo_ready, ONE + w_tile(g + 1, QKS_W[-1]))
                        transposed(bk_g, nb, SC if half == 0 else QC, 0)
                    pe.wait_ge(pvT_ready, ONE + n)
                    pe.wait_ge(qk_ready, 2 * n)
                    for a in range(PAIRS):
                        for e in range(2):
                            rows = slice(64 * e, 64 * e + 64)
                            mm = pe.matmul(bk_ab[e][:, 1, a, :], eT[b][rows, a, t], pvT[rows, a, :],
                                           start=True, stop=True)
                    mm.then_inc(ep_done, 1)
                    if more:
                        mm = transposed(bk_g, nb, SC if half == 0 else QC, 1)
                        mm.then_inc(s_done if half == 0 else q_done, 1)
                        if half == 1:
                            if not behind:
                                pe.wait_ge(y_added, ONE + n - 2)
                            for a in range(PAIRS):
                                mm = transposed(bk_v, nb, KC, a)
                            mm.then_inc(k_done, 1)

            every_step(pe, one_step)
            pe.wait_ge(ke_ready, chunk(NG - 1, NB - 1, 3))
            turn_o(NG - 1, NB - 1, 2)
            values(NG - 1, NB - 1, 3)
            pe.wait_ge(y_added, ONE + chunk(NG - 1, NB - 1, 1))
            project_y(NG - 1, NB - 1, 2)
            pe.wait_ge(oT_lo_ready, ONE + chunk(NG - 1, NB - 1, 2))
            turn_o(NG - 1, NB - 1, 3)
            pe.wait_ge(y_added, ONE + chunk(NG - 1, NB - 1, 2))
            project_y(NG - 1, NB - 1, 3)


def feed_forward(nc, consts, w13, w2f, x1t, yacc, ln, out):
    with ExitStack() as ctx:
        sb = lambda n, s, d=F32: ctx.enter_context(nc.sbuf_tensor(n, s, d))
        ps = lambda n, s: ctx.enter_context(nc.psum_tensor(n, s, F32))
        sem = lambda n: ctx.enter_context(nc.semaphore(n))
        NW = 3 * HT
        W13, W2 = 2 * KT, HT
        ident = sb("ident2", [P, P])
        stats, mv, var, rstd, spare = ln
        after = spare[:, 0:1]
        turned_x = [sb(f"turned_x{j}", [P, KT, TT * P]) for j in range(2)]
        w_hi, w_lo = sb("fw_hi", [P, NW, 512], F32R), sb("fw_lo", [P, NW, 512], F32R)
        w_stage, x_stage = sb("fw_stage", [P, NW, 512]), sb("fx_stage", [P, KT, 512])
        x_hi, x_lo = sb("fx_hi", [P, KT, 512], F32R), sb("fx_lo", [P, KT, 512], F32R)
        th = [sb(f"th{j}", [P, 512]) for j in range(2)]
        hid = [sb(f"hid{j}", [P, 512]) for j in range(2)]
        h_hi, h_lo = sb("h_hi", [P, HT, 512], F32R), sb("h_lo", [P, HT, 512], F32R)
        bk_gate = [ps(f"bk_gate{j}", [P, 512]) for j in range(2)]
        bk_up = [ps(f"bk_up{j}", [P, 512]) for j in range(2)]
        bk_y = [ps(f"bk_y{j}", [P, 512]) for j in range(TT)]

        id_in = sem("id_in")
        stat_ready, mv_ready, ln_step, normed = sem("stat_ready"), sem("mv_ready"), sem("ln_step"), sem("normed")
        turned, copied, copied_late = sem("turned"), sem("copied"), sem("copied_late")
        x1_stored = [sem(f"x1_stored{j}") for j in range(2)]
        w_staged = [sem(f"fw_staged{j}") for j in range(NW)]
        x_staged = [sem(f"fx_staged{j}") for j in range(KT)]
        w_hi_ready, w_lo_ready = sem("fw_hi_ready"), sem("fw_lo_ready")
        x_hi_ready, x_lo_ready = sem("fx_hi_ready"), sem("fx_lo_ready")
        gate_done, up_done, tanh_ready, act_ready, hid_ready = (sem(n) for n in (
            "fgate_done", "fup_done", "ftanh_ready", "fact_ready", "fhid_ready"))
        h_hi_ready, h_lo_ready = sem("h_hi_ready"), sem("h_lo_ready")
        y_done, y_added = sem("fy_done"), sem("fy_added")
        stat2_ready, mv2_ready, var2_ready, ln2_step, normed2 = (sem(n) for n in (
            "stat2_ready", "mv2_ready", "var2_ready", "ln2_step", "normed2"))
        out_stored = sem("out_stored")
        assert HT == KT == TT == 4 and NTILE == TT * NFS
        LATE = [T // P * (b + 1) - 2 + half for b in range(B) for half in range(2)]
        LAST = NHG - 1

        def x_tile(g, s, k):
            return KT * NFS * g + KT * s + (k + 1)

        def w_tile(g, w):
            return NW * g + (w + 1)

        def hidden(g, s, h):
            return HT * NFS * g + HT * s + (h + 1)

        block = ctx.enter_context(nc.Block())

        @block.sync
        def _(sp):
            def load_w(g, *tiles):
                for w in tiles:
                    if not (isinstance(g, int) and g == 0):
                        sp.wait_ge(w_lo_ready, w_tile(g, w) - NW)
                    src = w13[g, w] if w < W13 else w2f[HT * g + (w - W13)]
                    sp.dma_start(w_stage[:, w, :], src).then_inc(w_staged[w], 16)

            def load_x(g, s):
                sp.wait_ge(x1_stored[s % 2], 16 * (s // 2 + 1))
                for k in range(KT):
                    if not (isinstance(g, int) and g == s == 0):
                        sp.wait_ge(x_lo_ready, x_tile(g, s, k) - KT)
                    sp.dma_start(x_stage[:, k, :], x1t[s, :, k, :]).then_inc(x_staged[k], 16)

            sp.dma_start(ident[:, :], consts[:, 0:P]).then_inc(id_in, 16)
            load_w(0, *range(W13))
            load_x(0, 0)
            sp.wait_ge(x1_stored[1], 16 * NFS // 4)
            load_w(0, *range(W13, NW))
            with sp.Fori(0, LAST) as g:
                load_x(g, 1)
                load_w(g + 1, *range(NW))
                for s in range(2, NFS):
                    load_x(g, s)
                load_x(g + 1, 0)

            def store(s):
                sp.wait_ge(normed2, TT * (s + 1))
                sp.dma_start(out[:, TT * s:TT * s + TT, :], yacc[:, TT * s:TT * s + TT, :]).then_inc(out_stored, 16)

            for s in range(1, NFS):
                load_x(LAST, s)
                if s >= 2:
                    store(s - 2)
            store(NFS - 2)
            store(NFS - 1)
            sp.wait_ge(out_stored, 16 * NFS)

        @block.scalar
        def _(act):
            def w_high(g, *tiles):
                for w in tiles:
                    act.wait_ge(w_staged[w], 16 * g + 16)
                    act.activation(w_hi[:, w, :], w_stage[:, w, :], ACT.Copy).then_inc(w_hi_ready, 1)

            def x_high(g, s):
                for k in range(KT):
                    act.wait_ge(x_staged[k], 16 * (NFS * g + s) + 16)
                    act.activation(x_hi[:, k, :], x_stage[:, k, :], ACT.Copy).then_inc(x_hi_ready, 1)

            def turn_out(s):
                if s >= 2:
                    act.wait_ge(x1_stored[s % 2], 16 * (s // 2))
                for j in range(TT // 2):
                    act.wait_ge(turned, TT * s + j + 1)
                    act.activation(turned_x[s % 2][:, :, j * P:(j + 1) * P],
                                   bk_y[j][:, :].rearrange("p (k t) -> p k t", k=KT), ACT.Copy).then_inc(copied, 1)
                act.wait_ge(copied, TT // 2 * (s + 1))
                act.wait_ge(copied_late, TT // 2 * (s + 1))
                act.dma_start(x1t[s], turned_x[s % 2][:, :, :]).then_inc(x1_stored[s % 2], 16)

            turn_out(0)
            w_high(0, *range(KT))
            turn_out(1)
            w_high(0, *range(KT, W13))
            turn_out(2)
            x_high(0, 0)
            for s in range(3, NFS):
                turn_out(s)
            w_high(0, *range(W13, NW))

            def hidden_tiles(g, s):
                for h in range(HT):
                    n = hidden(g, s, h)
                    act.wait_ge(gate_done, n)
                    act.activation(th[h % 2][:, :], bk_gate[h % 2][:, :], ACT.Tanh, scale=0.5).then_inc(tanh_ready, 1)
                    act.wait_ge(hid_ready, ONE + n)
                    act.activation(h_hi[:, h, :], hid[h % 2][:, :], ACT.Copy).then_inc(h_hi_ready, 1)
                act.wait_ge(up_done, hidden(g, s, HT - 1))

            def steps_before_last(g):
                with act.Fori(0, NFS - 1) as s:
                    hidden_tiles(g, s)
                    x_high(g, s + 1)
                hidden_tiles(g, NFS - 1)

            with act.Fori(0, LAST) as g:
                steps_before_last(g)
                x_high(g + 1, 0)
                w_high(g + 1, *range(W13))
                act.wait_ge(y_done, TT * NFS * g + TT * NFS)
                w_high(g + 1, *range(W13, NW))
            steps_before_last(LAST)
            for j in range(2):
                act.wait_ge(x1_stored[j], 16 * NFS // 2)

        @block.gpsimd
        def _(pool):
            def x_low(g, s):
                for k in range(KT):
                    pool.wait_ge(x_hi_ready, x_tile(g, s, k))
                    pool.tensor_tensor(x_lo[:, k, :], x_stage[:, k, :], x_hi[:, k, :], ALU.subtract)\
                        .then_inc(x_lo_ready, 1)

            x_low(0, 0)

            def hidden_tiles(g, s):
                for h in range(HT):
                    n = hidden(g, s, h)
                    pool.wait_ge(h_hi_ready, n)
                    pool.tensor_tensor(h_lo[:, h, :], hid[h % 2][:, :], h_hi[:, h, :], ALU.subtract)\
                        .then_inc(h_lo_ready, 1)

            def steps_before_last(g):
                with pool.Fori(0, NFS - 1) as s:
                    hidden_tiles(g, s)
                    x_low(g, s + 1)
                hidden_tiles(g, NFS - 1)

            with pool.Fori(0, LAST) as g:
                steps_before_last(g)
                x_low(g + 1, 0)
            steps_before_last(LAST)

        @block.vector
        def _(dve):
            def w_low(g, *tiles):
                for w in tiles:
                    dve.wait_ge(w_hi_ready, w_tile(g, w))
                    dve.tensor_tensor(w_lo[:, w, :], w_stage[:, w, :], w_hi[:, w, :], ALU.subtract)\
                        .then_inc(w_lo_ready, 1)

            def copy_turned(s):
                if s >= 2:
                    dve.wait_ge(x1_stored[s % 2], 16 * (s // 2))
                for j in range(TT // 2, TT):
                    dve.wait_ge(turned, TT * s + j + 1)
                    dve.tensor_copy(turned_x[s % 2][:, :, j * P:(j + 1) * P],
                                    bk_y[j][:, :].rearrange("p (k t) -> p k t", k=KT)).then_inc(copied_late, 1)

            copy_turned(0)
            for j, t in enumerate(LATE):
                dve.bn_stats(stats[:, j, :], yacc[:, t, :]).then_inc(stat_ready, 1)
            copy_turned(1)
            for j in range(4):
                dve.wait_ge(stat_ready, j + 1)
                dve.bn_aggr(mv[:, j, :], stats[:, j, :]).then_inc(mv_ready, 1)
            dve.wait_ge(mv_ready, 4)
            dve.tensor_scalar(var[:, :], mv[:, :, 1], 1.0, EPS, ALU.mult, ALU.add).then_inc(ln_step, 1)
            dve.wait_ge(ln_step, 1)
            rsqrt(dve, var[:, :], rstd[:, :], spare[:, :], ln_step, 1)
            dve.wait_ge(ln_step, 1 + NEWTON)
            for j, t in enumerate(LATE):
                dve.tensor_scalar(yacc[:, t, :], yacc[:, t, :], mv[:, j, 0:1], rstd[:, j:j + 1],
                                  ALU.subtract, ALU.mult).then_inc(normed, 1)
            copy_turned(2)
            w_low(0, *range(KT))
            copy_turned(3)
            w_low(0, *range(KT, W13))
            for s in range(4, NFS):
                copy_turned(s)
            w_low(0, *range(W13, NW))

            def hidden_tiles(g, s):
                for h in range(HT):
                    n = hidden(g, s, h)
                    dve.wait_ge(tanh_ready, n)
                    dve.scalar_tensor_tensor(out=th[h % 2][:, :], in0=th[h % 2][:, :], scalar=1.0,
                                             in1=bk_gate[h % 2][:, :], op0=ALU.add, op1=ALU.mult)\
                        .then_inc(act_ready, 1)
                    dve.wait_ge(act_ready, n)
                    dve.wait_ge(up_done, n)
                    dve.wait_ge(h_lo_ready, ONE + (n - 2 if h >= 2 else HT * NFS * g + HT * s))
                    dve.tensor_tensor(hid[h % 2][:, :], th[h % 2][:, :], bk_up[h % 2][:, :], ALU.mult)\
                        .then_inc(hid_ready, 1)

            def add_y(g, s):
                for t in range(TT):
                    dve.wait_ge(y_done, TT * NFS * g + TT * s + (t + 1))
                    dve.tensor_tensor(yacc[:, TT * s + t, :], yacc[:, TT * s + t, :], bk_y[t][:, :], ALU.add)\
                        .then_inc(y_added, 1)

            with dve.Fori(0, LAST) as g:
                with dve.Fori(0, NFS - 1) as s:
                    hidden_tiles(g, s)
                    add_y(g, s)
                hidden_tiles(g, NFS - 1)
                w_low(g + 1, *range(W13))
                add_y(g, NFS - 1)
                w_low(g + 1, *range(W13, NW))
            with dve.Fori(0, NFS) as s:
                hidden_tiles(LAST, s)
                add_y(LAST, s)
                dve.wait_ge(y_added, ONE + TT * NFS * LAST + TT * s + TT)
                dve.memset(after, 0.0)
                for t in range(TT):
                    dve.bn_stats(stats[:, t, :], yacc[:, TT * s + t, :]).then_inc(stat2_ready, 1)
                dve.wait_ge(stat2_ready, TT * s + TT)
                dve.memset(after, 0.0)
                for t in range(TT):
                    dve.bn_aggr(mv[:, t, :], stats[:, t, :]).then_inc(mv2_ready, 1)
                dve.wait_ge(mv2_ready, TT * s + TT)
                dve.tensor_scalar(var[:, :], mv[:, :, 1], 1.0, EPS, ALU.mult, ALU.add).then_inc(var2_ready, 1)
                dve.wait_ge(var2_ready, s + 1)
                rsqrt(dve, var[:, :], rstd[:, :], spare[:, :], ln2_step, NEWTON * s)
                dve.wait_ge(ln2_step, NEWTON * s + NEWTON)
                for t in range(TT):
                    dve.tensor_scalar(yacc[:, TT * s + t, :], yacc[:, TT * s + t, :], mv[:, t, 0:1], rstd[:, t:t + 1],
                                      ALU.subtract, ALU.mult).then_inc(normed2, 1)

        @block.tensor
        def _(pe):
            for started in (hid_ready, h_lo_ready, y_added):
                pe.sem_inc(started, ONE)
            pe.wait_ge(id_in, 16)
            for n in range(NTILE):
                if n in LATE:
                    pe.wait_ge(normed, LATE.index(n) + 1)
                if n >= TT:
                    pe.wait_ge(copied if n % TT < TT // 2 else copied_late, TT // 2 * (n // TT - 1) + n % 2 + 1)
                for k in range(KT):
                    mm = pe.transpose(bk_y[n % TT][:, k * P:(k + 1) * P], yacc[:, n, k * P:(k + 1) * P], ident[:, :])
                mm.then_inc(turned, 1)
            with pe.Fori(0, NHG) as g:
                with pe.Fori(0, NFS) as s:
                    pe.wait_ge(w_lo_ready, w_tile(g, W13 - 1))
                    pe.wait_ge(x_lo_ready, x_tile(g, s, KT - 1))
                    for h in range(HT):
                        n = hidden(g, s, h)
                        c = slice(h * P, h * P + P)
                        pe.wait_ge(hid_ready, ONE + (n - 2 if h >= 2 else HT * NFS * g + HT * s))
                        for bank, w0, done in ((bk_gate, 0, gate_done), (bk_up, KT, up_done)):
                            split_product(pe, bank[h % 2][:, :],
                                          [((w_hi[:, w0 + k, c], w_lo[:, w0 + k, c]), (x_hi[:, k, :], x_lo[:, k, :]))
                                           for k in range(KT)]).then_inc(done, 1)
                    pe.wait_ge(copied, NTILE // 2)
                    pe.wait_ge(copied_late, NTILE // 2)
                    pe.wait_ge(y_added, ONE + TT * NFS * g + TT * s)
                    pe.wait_ge(w_lo_ready, w_tile(g, NW - 1))
                    for h in range(HT):
                        pe.wait_ge(h_lo_ready, ONE + hidden(g, s, h))
                        for t in range(TT):
                            c = slice(t * P, t * P + P)
                            w = W13 + h
                            pe.matmul(bk_y[t][:, :], h_hi[:, h, c], w_hi[:, w, :], start=(h == 0), stop=False)
                            pe.matmul(bk_y[t][:, :], h_hi[:, h, c], w_lo[:, w, :], start=False, stop=False)
                            mm = pe.matmul(bk_y[t][:, :], h_lo[:, h, c], w_hi[:, w, :], start=False, stop=(h == HT - 1))
                            if h == HT - 1:
                                mm.then_inc(y_done, 1)


def program(nc, consts, x_tok, xt, wt, wo, gw, w13, w2t, w2f, x1t, out):
    with ExitStack() as ctx:
        yacc = ctx.enter_context(nc.sbuf_tensor("yacc", [P, NTILE, D], F32))
        ln = [ctx.enter_context(nc.sbuf_tensor(n, s, F32)) for n, s in (
            ("stats", [P, 4, 6]), ("mv", [P, 4, 2]), ("var", [P, 4]), ("rstd", [P, 4]), ("spare", [P, 4]))]
        out_tok = out.rearrange("b (n p) d -> p (b n) d", p=P)
        attention(nc, consts, x_tok.rearrange("b (n p) d -> p (b n) d", p=P), xt, wt, wo, gw,
                  w2t, w2f, yacc, ln)
        feed_forward(nc, consts, w13, w2f, x1t, yacc, ln, out_tok)


def kernel(**inputs):
    import concourse.bacc as _bacc
    from concourse.bass_utils import run_bass_kernel_spmd as _run

    f32 = np.float32
    x = np.asarray(inputs["L0_attn_hidden_states"])
    wq, wk, wv, wg, ws = (np.asarray(inputs["L0_attn_W" + c]) for c in "qkvgs")
    w1, w2, w3 = (np.asarray(inputs["L0_ffn_W" + c]) for c in "123")

    def tiles(w, n):
        return np.ascontiguousarray(w.reshape(KT, P, n, 512).transpose(0, 2, 1, 3))

    xt = np.ascontiguousarray(x.reshape(B, NB, ST, 2, 2, P).transpose(0, 1, 3, 5, 4, 2)).reshape(B, NB, 2, P, 512)
    groups = []
    for g in range(NG):
        side = np.concatenate([wq[:, g * HG * DK:(g + 1) * HG * DK], wk[:, g * HG * DK:(g + 1) * HG * DK],
                               ws[:, g * HG * M:(g + 1) * HG * M]], axis=1)
        qks = side.reshape(KT, P, QKS).transpose(1, 0, 2).reshape(P, len(QKS_W), 512).transpose(1, 0, 2)
        v, gate = (w[:, g * HG * DV:(g + 1) * HG * DV].reshape(KT, P, 512) for w in (wv, wg))
        groups.append(np.concatenate([qks, v, gate]))
    wt = np.ascontiguousarray(np.stack(groups))
    wo = np.ascontiguousarray(np.asarray(inputs["L0_attn_Wo"]).reshape(NG, HG, P, D))
    gw = np.ascontiguousarray(np.asarray(inputs["L0_attn_g_norm_weight"]).reshape(P, 1))
    w13 = np.ascontiguousarray(np.stack([w.T.reshape(KT, P, NHG, 512).transpose(2, 0, 1, 3) for w in (w1, w3)],
                                        axis=1)).reshape(NHG, 2 * KT, P, 512)
    w2t = np.ascontiguousarray(w2.T.reshape(FF // P, P, 4, P).transpose(2, 1, 0, 3))
    had = np.array([[1.0]], f32)
    while had.shape[0] < P:
        had = np.block([[had, had], [had, -had]])
    consts = np.concatenate([np.eye(P, dtype=f32), np.triu(np.ones((P, P), f32)), had, -had], axis=1).astype(f32)

    nc = _bacc.Bacc("TRN2", target_bir_lowering=False, num_devices=1)
    arrays = {"consts": consts, "x_tok": np.ascontiguousarray(x), "xt": xt, "wt": wt, "wo": wo, "gw": gw,
              "w13": w13, "w2t": w2t}
    aps = [nc.dram_tensor(n, a.shape, mybir.dt.from_np(a.dtype), kind="ExternalInput").ap() for n, a in arrays.items()]
    w2f = nc.dram_tensor("w2f", (FF // P, P, D), F32, kind="Internal").ap()
    x1t = nc.dram_tensor("x1t", (NFS, P, KT, TT * P), F32, kind="Internal").ap()
    out = nc.dram_tensor("out", (B, T, D), F32, kind="ExternalOutput").ap()
    program(nc, *aps, w2f, x1t, out)
    r = _run(nc, [arrays], core_ids=[0])
    return r.results[0]["out"]
```
